# Optimizing a Trainium2 kernel written in Bass

```python
import numpy as np
import jax
import jax.numpy as jnp

def _softmax(x, axis=-1):
    return jax.nn.softmax(x, axis=axis)

def _gelu(x):
    return jax.nn.gelu(x, approximate=True)

def _silu(x):
    return jax.nn.silu(x)

def _sigmoid(x):
    return jax.nn.sigmoid(x)

def _layernorm(x, axis=-1, eps=1e-05):
    m = jnp.mean(x, axis=axis, keepdims=True)
    v = jnp.var(x, axis=axis, keepdims=True)
    return (x - m) / jnp.sqrt(v + eps)

def _scatter_add(tgt, idx, src, axis=0):
    return tgt.at[idx].add(src)

def _segment_sum(src, seg, n):
    return jax.ops.segment_sum(src, seg, n)
kernel_name = 'mk_gnn_preln_d4_gnn_r8_c46b52'

def setup_inputs(seed: int=0):
    np.random.seed(seed)
    _w = jnp.asarray

    def _rec_inputs():
        import jax
        import jax.numpy as jnp
        _gk = jax.random.key(seed)
        x = -0.0005121 + 1.001 * jax.random.normal(jax.random.fold_in(_gk, 1), (12500, 64), jnp.float32)
        _s = jax.random.randint(jax.random.fold_in(_gk, 2), (100000,), 0, 12500, jnp.int32)
        _d = jax.random.randint(jax.random.fold_in(_gk, 3), (100000,), 0, 12500, jnp.int32)
        _loop = jnp.arange(12500, dtype=jnp.int32)
        src = jnp.concatenate([_s, _d, _loop])
        dst = jnp.concatenate([_d, _s, _loop])
        _o = jnp.argsort(dst, stable=True)
        src = src[_o]
        dst = dst[_o]
        edge_attr_16 = 6.40344e-05 + 1.00026 * jax.random.normal(jax.random.fold_in(_gk, 12), (212500, 16), jnp.float32)
        edge_attr_2 = jax.random.uniform(jax.random.fold_in(_gk, 13), (212500, 2), jnp.float32, 0.0, 0.999999)
        edge_attr_32 = 0.000216709 + 1.00012 * jax.random.normal(jax.random.fold_in(_gk, 14), (212500, 32), jnp.float32)
        return (x, src, dst, edge_attr_16, edge_attr_2, edge_attr_32)
    x, src, dst, edge_attr_16, edge_attr_2, edge_attr_32 = _rec_inputs()

    def _L0_gnn_setup():
        import jax, jax.numpy as jnp
        import numpy as np
        N_NODES = 6250
        N_EDGES = 100000
        IN_C = 64
        OUT_C = 64
        DIM = 2
        NUM_LAYERS = 2
        KS = 5
        K2 = KS ** DIM
        S = 2 ** DIM
        CAT_IN = IN_C + NUM_LAYERS * OUT_C

        def spline_basis(pseudo):
            v = pseudo * (KS - 1)
            base = jnp.floor(v)
            frac = v - base
            base = base.astype(jnp.int32)
            bits = jnp.arange(S, dtype=jnp.int32)[:, None] >> jnp.arange(DIM, dtype=jnp.int32)[None, :] & 1
            b = jnp.where(bits[None].astype(bool), frac[:, None, :], 1.0 - frac[:, None, :])
            basis = jnp.prod(b, axis=-1)
            idx = jnp.clip(base[:, None, :] + bits[None], 0, KS - 1)
            strides = KS ** jnp.arange(DIM, dtype=jnp.int32)
            widx = jnp.sum(idx * strides, axis=-1)
            return (basis, widx)

        def spline_conv(h, src, dst, basis, widx, W, root, bias, n_nodes):
            xw = jnp.einsum('ni,kio->nko', h, W)
            g = xw[src[:, None], widx]
            msg = jnp.einsum('es,eso->eo', basis, g)
            agg = jax.ops.segment_sum(msg, dst, num_segments=n_nodes)
            deg = jax.ops.segment_sum(jnp.ones(msg.shape[0], h.dtype), dst, num_segments=n_nodes)
            out = agg / jnp.maximum(deg, 1.0)[:, None]
            return out + h @ root + bias
        key = jax.random.key(seed)
        ks = jax.random.split(key, 8)
        x = jax.random.normal(ks[0], (N_NODES, IN_C), dtype=jnp.float32)
        edge_index = jax.random.randint(ks[1], (2, N_EDGES), 0, N_NODES, dtype=jnp.int32)
        edge_attr = jax.random.uniform(ks[2], (N_EDGES, DIM), dtype=jnp.float32)
        w_scale = (1.0 / (IN_C * S)) ** 0.5
        weights = jax.random.normal(ks[3], (NUM_LAYERS, K2, IN_C, OUT_C), dtype=jnp.float32) * w_scale
        roots = jax.random.normal(ks[4], (NUM_LAYERS, IN_C, OUT_C), dtype=jnp.float32) * (1.0 / IN_C) ** 0.5
        biases = jnp.zeros((NUM_LAYERS, OUT_C), dtype=jnp.float32)
        final_w = jax.random.normal(ks[5], (OUT_C, CAT_IN), dtype=jnp.float32) * (1.0 / CAT_IN) ** 0.5
        final_b = jnp.zeros((OUT_C,), dtype=jnp.float32)
        return {'x': x, 'edge_index': edge_index, 'edge_attr': edge_attr, 'weights': weights, 'roots': roots, 'biases': biases, 'final_w': final_w, 'final_b': final_b}
    _L0_gnn_all = _L0_gnn_setup()
    _L0_gnn_in = {k: v for k, v in _L0_gnn_all.items() if k in ('weights', 'roots', 'biases', 'final_w', 'final_b')}
    del _L0_gnn_all

    def _L1_gnn_setup():
        import jax, jax.numpy as jnp
        import numpy as np
        N_NODES = 12500
        N_EDGES = 200000
        D_FEAT = 64
        key = jax.random.key(seed)
        k1, k2 = jax.random.split(key)
        x = jax.random.normal(k1, (N_NODES, D_FEAT), dtype=jnp.float32)
        edge_index = jax.random.randint(k2, (2, N_EDGES), 0, N_NODES, dtype=jnp.int64)
        return {'x': x, 'edge_index': edge_index}
    _L1_gnn_all = _L1_gnn_setup()
    _L1_gnn_in = {k: v for k, v in _L1_gnn_all.items() if k in ()}
    del _L1_gnn_all

    def _L2_gnn_setup():
        import jax, jax.numpy as jnp
        import numpy as np
        N_NODES = 6250
        N_EDGES = 100000
        D_NODE = 64
        D_EDGE = 32
        D_HID = 128

        def _mlp(x, W1, b1, W2, b2):
            return jax.nn.relu(x @ W1 + b1) @ W2 + b2
        key = jax.random.key(seed)
        ks = jax.random.split(key, 12)
        inp = {'nodes': jax.random.normal(ks[0], (N_NODES, D_NODE), dtype=jnp.float32), 'row': jax.random.randint(ks[1], (N_EDGES,), 0, N_NODES, dtype=jnp.int32), 'col': jax.random.randint(ks[2], (N_EDGES,), 0, N_NODES, dtype=jnp.int32), 'edge_features': jax.random.normal(ks[3], (N_EDGES, D_EDGE), dtype=jnp.float32)}
        d_in_msg = 2 * D_NODE + D_EDGE
        inp['mW1'] = jax.random.normal(ks[4], (d_in_msg, D_HID), dtype=jnp.float32) / np.sqrt(d_in_msg)
        inp['mb1'] = jnp.zeros((D_HID,), dtype=jnp.float32)
        inp['mW2'] = jax.random.normal(ks[5], (D_HID, D_NODE), dtype=jnp.float32) / np.sqrt(D_HID)
        inp['mb2'] = jnp.zeros((D_NODE,), dtype=jnp.float32)
        d_in_upd = 2 * D_NODE
        inp['uW1'] = jax.random.normal(ks[6], (d_in_upd, D_HID), dtype=jnp.float32) / np.sqrt(d_in_upd)
        inp['ub1'] = jnp.zeros((D_HID,), dtype=jnp.float32)
        inp['uW2'] = jax.random.normal(ks[7], (D_HID, D_NODE), dtype=jnp.float32) / np.sqrt(D_HID)
        inp['ub2'] = jnp.zeros((D_NODE,), dtype=jnp.float32)
        return inp
    _L2_gnn_all = _L2_gnn_setup()
    _L2_gnn_in = {k: v for k, v in _L2_gnn_all.items() if k in ('mW1', 'mb1', 'mW2', 'mb2', 'uW1', 'ub1', 'uW2', 'ub2')}
    del _L2_gnn_all

    def _L3_gnn_setup():
        import jax, jax.numpy as jnp
        import numpy as np
        N, E, IN, H, EC = (6250, 100000, 64, 64, 16)
        CAT = 2 * IN + EC

        def _mp_layer(x, src_f, dst_f, ea_f, W, b):
            n = x.shape[0]
            m = jnp.concatenate([x[dst_f], x[src_f], ea_f], axis=1) @ W.T + b
            agg = jax.ops.segment_sum(m, dst_f, num_segments=n)
            return jax.nn.relu(agg)

        def _batchnorm(x, gamma, beta, eps=1e-05):
            mu = x.mean(axis=0)
            var = x.var(axis=0)
            return (x - mu) * jax.lax.rsqrt(var + eps) * gamma + beta
        key = jax.random.key(seed)
        ks = jax.random.split(key, 8)
        s = 1.0 / np.sqrt(CAT)
        return {'x': jax.random.normal(ks[0], (N, IN), jnp.float32), 'edge_src': jax.random.randint(ks[1], (E,), 0, N, jnp.int32), 'edge_dst': jax.random.randint(ks[2], (E,), 0, N, jnp.int32), 'edge_attr': jax.random.normal(ks[3], (E, EC), jnp.float32), 'W0': jax.random.normal(ks[4], (H, CAT), jnp.float32) * s, 'b0': jnp.zeros((H,), jnp.float32), 'W1': jax.random.normal(ks[5], (H, CAT), jnp.float32) * s, 'b1': jnp.zeros((H,), jnp.float32), 'W2': jax.random.normal(ks[6], (H, CAT), jnp.float32) * s, 'b2': jnp.zeros((H,), jnp.float32), 'g0': jnp.ones((H,), jnp.float32), 'be0': jnp.zeros((H,), jnp.float32), 'g1': jnp.ones((H,), jnp.float32), 'be1': jnp.zeros((H,), jnp.float32)}
    _L3_gnn_all = _L3_gnn_setup()
    _L3_gnn_in = {k: v for k, v in _L3_gnn_all.items() if k in ('W0', 'b0', 'W1', 'b1', 'W2', 'b2', 'g0', 'be0', 'g1', 'be1')}
    del _L3_gnn_all
    return {'x': x, 'src': src, 'dst': dst, 'edge_attr_16': edge_attr_16, 'edge_attr_2': edge_attr_2, 'edge_attr_32': edge_attr_32, 'L0_gnn_weights': _L0_gnn_in['weights'], 'L0_gnn_roots': _L0_gnn_in['roots'], 'L0_gnn_biases': _L0_gnn_in['biases'], 'L0_gnn_final_w': _L0_gnn_in['final_w'], 'L0_gnn_final_b': _L0_gnn_in['final_b'], 'L2_gnn_mW1': _L2_gnn_in['mW1'], 'L2_gnn_mb1': _L2_gnn_in['mb1'], 'L2_gnn_mW2': _L2_gnn_in['mW2'], 'L2_gnn_mb2': _L2_gnn_in['mb2'], 'L2_gnn_uW1': _L2_gnn_in['uW1'], 'L2_gnn_ub1': _L2_gnn_in['ub1'], 'L2_gnn_uW2': _L2_gnn_in['uW2'], 'L2_gnn_ub2': _L2_gnn_in['ub2'], 'L3_gnn_W0': _L3_gnn_in['W0'], 'L3_gnn_b0': _L3_gnn_in['b0'], 'L3_gnn_W1': _L3_gnn_in['W1'], 'L3_gnn_b1': _L3_gnn_in['b1'], 'L3_gnn_W2': _L3_gnn_in['W2'], 'L3_gnn_b2': _L3_gnn_in['b2'], 'L3_gnn_g0': _L3_gnn_in['g0'], 'L3_gnn_be0': _L3_gnn_in['be0'], 'L3_gnn_g1': _L3_gnn_in['g1'], 'L3_gnn_be1': _L3_gnn_in['be1']}

def reference(x, src, dst, edge_attr_16, edge_attr_2, edge_attr_32, L0_gnn_weights, L0_gnn_roots, L0_gnn_biases, L0_gnn_final_w, L0_gnn_final_b, L2_gnn_mW1, L2_gnn_mb1, L2_gnn_mW2, L2_gnn_mb2, L2_gnn_uW1, L2_gnn_ub1, L2_gnn_uW2, L2_gnn_ub2, L3_gnn_W0, L3_gnn_b0, L3_gnn_W1, L3_gnn_b1, L3_gnn_W2, L3_gnn_b2, L3_gnn_g0, L3_gnn_be0, L3_gnn_g1, L3_gnn_be1):
    import jax
    import jax.numpy as jnp

    def _L0_gnn_ref(x, edge_index, edge_attr, weights, roots, biases, final_w, final_b):
        import jax, jax.numpy as jnp
        import numpy as np
        N_NODES = 6250
        N_EDGES = 100000
        IN_C = 64
        OUT_C = 64
        DIM = 2
        NUM_LAYERS = 2
        KS = 5
        K2 = KS ** DIM
        S = 2 ** DIM
        CAT_IN = IN_C + NUM_LAYERS * OUT_C

        def spline_basis(pseudo):
            v = pseudo * (KS - 1)
            base = jnp.floor(v)
            frac = v - base
            base = base.astype(jnp.int32)
            bits = jnp.arange(S, dtype=jnp.int32)[:, None] >> jnp.arange(DIM, dtype=jnp.int32)[None, :] & 1
            b = jnp.where(bits[None].astype(bool), frac[:, None, :], 1.0 - frac[:, None, :])
            basis = jnp.prod(b, axis=-1)
            idx = jnp.clip(base[:, None, :] + bits[None], 0, KS - 1)
            strides = KS ** jnp.arange(DIM, dtype=jnp.int32)
            widx = jnp.sum(idx * strides, axis=-1)
            return (basis, widx)

        def spline_conv(h, src, dst, basis, widx, W, root, bias, n_nodes):
            xw = jnp.einsum('ni,kio->nko', h, W)
            g = xw[src[:, None], widx]
            msg = jnp.einsum('es,eso->eo', basis, g)
            agg = jax.ops.segment_sum(msg, dst, num_segments=n_nodes)
            deg = jax.ops.segment_sum(jnp.ones(msg.shape[0], h.dtype), dst, num_segments=n_nodes)
            out = agg / jnp.maximum(deg, 1.0)[:, None]
            return out + h @ root + bias
        n = x.shape[0]
        src, dst = (edge_index[0], edge_index[1])
        basis, widx = spline_basis(edge_attr)
        xs = [x]
        h = x
        for l in range(NUM_LAYERS):
            h = jax.nn.relu(spline_conv(h, src, dst, basis, widx, weights[l], roots[l], biases[l], n))
            xs.append(h)
        cat = jnp.concatenate(xs, axis=-1)
        return cat @ final_w.T + final_b

    def _L1_gnn_ref(x, edge_index):
        import jax, jax.numpy as jnp
        import numpy as np
        N_NODES = 12500
        N_EDGES = 200000
        D_FEAT = 64
        from_, to_ = (edge_index[0], edge_index[1])
        n = x.shape[0]
        deg = jax.ops.segment_sum(jnp.ones_like(to_, dtype=x.dtype), to_, num_segments=n)
        deg_inv = jnp.where(deg > 0, 1.0 / jnp.sqrt(deg), 0.0)
        norm = deg_inv[from_] * deg_inv[to_]
        m_j = norm[:, None] * x[from_]
        out = jax.ops.segment_sum(m_j, to_, num_segments=n)
        return out

    def _L2_gnn_ref(nodes, row, col, edge_features, mW1, mb1, mW2, mb2, uW1, ub1, uW2, ub2):
        import jax, jax.numpy as jnp
        import numpy as np
        N_NODES = 6250
        N_EDGES = 100000
        D_NODE = 64
        D_EDGE = 32
        D_HID = 128

        def _mlp(x, W1, b1, W2, b2):
            return jax.nn.relu(x @ W1 + b1) @ W2 + b2
        msg_in = jnp.concatenate([nodes[row], nodes[col], edge_features], axis=-1)
        messages = _mlp(msg_in, mW1, mb1, mW2, mb2)
        aggregated = jax.ops.segment_sum(messages, col, num_segments=nodes.shape[0])
        upd_in = jnp.concatenate([nodes, aggregated], axis=-1)
        return _mlp(upd_in, uW1, ub1, uW2, ub2)

    def _L3_gnn_ref(x, edge_src, edge_dst, edge_attr, W0, b0, W1, b1, W2, b2, g0, be0, g1, be1):
        import jax, jax.numpy as jnp
        import numpy as np
        N, E, IN, H, EC = (6250, 100000, 64, 64, 16)
        CAT = 2 * IN + EC

        def _mp_layer(x, src_f, dst_f, ea_f, W, b):
            n = x.shape[0]
            m = jnp.concatenate([x[dst_f], x[src_f], ea_f], axis=1) @ W.T + b
            agg = jax.ops.segment_sum(m, dst_f, num_segments=n)
            return jax.nn.relu(agg)

        def _batchnorm(x, gamma, beta, eps=1e-05):
            mu = x.mean(axis=0)
            var = x.var(axis=0)
            return (x - mu) * jax.lax.rsqrt(var + eps) * gamma + beta
        n = x.shape[0]
        loop = jnp.arange(n, dtype=edge_src.dtype)
        src_f = jnp.concatenate([edge_src, loop])
        dst_f = jnp.concatenate([edge_dst, loop])
        ea_f = jnp.concatenate([edge_attr, jnp.ones((n, edge_attr.shape[1]), edge_attr.dtype)], axis=0)
        h = _mp_layer(x, src_f, dst_f, ea_f, W0, b0)
        h = jax.nn.relu(_batchnorm(h, g0, be0))
        h = _mp_layer(h, src_f, dst_f, ea_f, W1, b1)
        h = jax.nn.relu(_batchnorm(h, g1, be1))
        h = _mp_layer(h, src_f, dst_f, ea_f, W2, b2)
        return h
    edge_index = jnp.stack([src, dst])
    h = jnp.maximum(_layernorm(x, axis=-1), 0.0)
    x = x + _L0_gnn_ref(h, edge_index, edge_attr_2, L0_gnn_weights, L0_gnn_roots, L0_gnn_biases, L0_gnn_final_w, L0_gnn_final_b)
    h = jnp.maximum(_layernorm(x, axis=-1), 0.0)
    x = x + _L1_gnn_ref(h, edge_index)
    h = jnp.maximum(_layernorm(x, axis=-1), 0.0)
    x = x + _L2_gnn_ref(h, src, dst, edge_attr_32, L2_gnn_mW1, L2_gnn_mb1, L2_gnn_mW2, L2_gnn_mb2, L2_gnn_uW1, L2_gnn_ub1, L2_gnn_uW2, L2_gnn_ub2)
    h = jnp.maximum(_layernorm(x, axis=-1), 0.0)
    x = x + _L3_gnn_ref(h, src, dst, edge_attr_16, L3_gnn_W0, L3_gnn_b0, L3_gnn_W1, L3_gnn_b1, L3_gnn_W2, L3_gnn_b2, L3_gnn_g0, L3_gnn_be0, L3_gnn_g1, L3_gnn_be1)
    return x

_drawn_inputs = setup_inputs


def setup_inputs(seed=0):
    import zlib

    import numpy as np

    out = dict(_drawn_inputs(seed))
    spreads = {'L0_gnn_biases': (0.0, 0.1),
     'L0_gnn_final_b': (0.0, 0.1),
     'L2_gnn_mb1': (0.0, 0.1),
     'L2_gnn_mb2': (0.0, 0.1),
     'L2_gnn_ub1': (0.0, 0.1),
     'L2_gnn_ub2': (0.0, 0.1),
     'L3_gnn_b0': (0.0, 0.1),
     'L3_gnn_b1': (0.0, 0.1),
     'L3_gnn_b2': (0.0, 0.1),
     'L3_gnn_g0': (1.0, 0.2),
     'L3_gnn_be0': (0.0, 0.1),
     'L3_gnn_g1': (1.0, 0.2),
     'L3_gnn_be1': (0.0, 0.1)}
    factors = {}
    for name, (base, spread) in spreads.items():
        noise = np.random.default_rng([zlib.crc32(name.encode()), seed]).standard_normal(out[name].shape)
        drawn = base * np.exp(spread * noise) if base else spread * noise
        out[name] = jnp.asarray(drawn.astype(out[name].dtype))
    for name, factor in factors.items():
        out[name] = (out[name] * factor).astype(out[name].dtype)
    return out
```

```python
import concourse.bass as bass
from concourse import mybir
from contextlib import ExitStack

P = 128
F = 64
TILES = 15
CHUNKS = 3
NB_STEP = 9
CELLS = 16
CELL_W = 4 * F
CAT_E = 17
FEAT_E = 32
HID = 128
EPS = 1e-5

F32 = mybir.dt.float32
I32 = mybir.dt.int32
ALU = mybir.AluOpType
ACT = mybir.ActivationFunctionType
AX = mybir.AxisListType


class Sizes:

    def __init__(self, nodes, edges):
        self.nodes = nodes
        self.groups = -(-edges // (TILES * P))
        self.tiles = self.groups * TILES
        step = P * NB_STEP
        self.rows = -(-(nodes + 1 + P) // step) * step
        self.blocks = self.rows // P
        self.steps = self.blocks // NB_STEP


class Route:

    def __init__(self, name, groups, chunks, chunk_tiles, sem):
        self.name, self.fast = name, name == "fast"
        self.groups, self.chunks, self.chunk_tiles = groups, chunks, chunk_tiles
        self.oh_ready = sem("oh_ready")
        self.chunk_done = sem("chunk_done")
        self.win_staged = sem("win_staged")
        self.slots_staged = sem("slots_staged")
        self.scattered = sem("scattered")
        self.prod_ready = sem("prod_ready")
        self.ea_staged = sem("ea_staged")
        self.ea_scattered = sem("ea_scattered")
        self.oh_turned = sem("oh_turned")
        self.oht_ready = sem("oht_ready")
        self.hid_done = sem("hid_done")
        self.hid_added = sem("hid_added")
        self.hid_ready = sem("hid_ready")
        self.qidx_in = sem("qidx_in")
        self.q_in = sem("q_in")
        self.q_copied = sem("q_copied")
        self.row_staged = sem("row_staged")
        self.row_ready = sem("row_ready")
        self.idx_in = [sem(f"idx_in{c}") for c in range(chunks)]
        self.gathered = [sem(f"gathered{c}") for c in range(chunks)]
        self.ea_in = [sem(f"ea_in{c}") for c in range(chunks)]
        self.ef_in = [sem(f"ef_in{c}") for c in range(chunks)]


class Links:

    def __init__(self, dve, done, step, per_step):
        self.dve, self.done, self.base, self.per_step, self.n = dve, done, step * per_step, per_step, 0

    def __call__(self, instruction):
        self.n += 1
        instruction.then_inc(self.done, 1)
        self.dve.wait_ge(self.done, self.base + self.n)

    def end(self):
        assert self.n == self.per_step, (self.n, self.per_step)


def gnn_program(nc, z, t):
    with ExitStack() as ctx:
        def sb(name, shape, dt=F32):
            return ctx.enter_context(nc.sbuf_tensor(name, shape, dt))

        def dram(name, shape, dt=F32):
            return nc.dram_tensor(name, shape, dt).ap()

        ctx.enter_context(nc.allow_non_contiguous_dma(reason="columns of 128 indices"))
        named = {}

        def sem(name):
            if name not in named:
                named[name] = ctx.enter_context(nc.semaphore(name))
            return named[name]

        t_cell = dram("t_cell", (z.rows * CELLS, CELL_W))
        t_gcn = dram("t_gcn", (z.rows, F))
        t_p = dram("t_p", (z.rows, HID))
        t_q = dram("t_q", (z.rows, HID))
        t_mp = [dram(f"t_mp{l}", (z.rows, F)) for l in range(3)]
        cell_idx = dram("cell_idx", (P, z.tiles), I32)
        acc_ea = dram("acc_ea", (z.rows, CAT_E))
        passes = [("spline", t_cell, CELL_W, dram("acc0", (z.rows, F))),
                  ("spline", t_cell, CELL_W, dram("acc1", (z.rows, F))),
                  ("sum", t_gcn, F, dram("acc2", (z.rows, F))),
                  ("mlp", t_p, HID, dram("acc3", (z.rows, HID))),
                  ("sum", t_mp[0], F, dram("acc4", (z.rows, F))),
                  ("sum", t_mp[1], F, dram("acc5", (z.rows, F))),
                  ("sum", t_mp[2], F, dram("acc6", (z.rows, F)))]

        X = sb("X", [P, z.blocks, F])
        H = sb("H", [P, z.blocks, F])
        COEF = sb("COEF", [P, max(z.tiles * 4, z.blocks * F)])
        coef = COEF[:, 0:z.tiles * 4].rearrange("p (t s) -> p t s", s=4)
        D = COEF[:, 0:z.blocks * F].rearrange("p (b f) -> p b f", f=F)
        DSTF = sb("DSTF", [P, z.tiles])
        REL = sb("REL", [P, z.tiles])
        SLOTF = sb("SLOTF", [P, z.tiles])
        SLOTI = sb("SLOTI", [P, z.tiles], I32)
        S17 = sb("S17", [P, z.blocks, CAT_E])
        INVD = sb("INVD", [P, z.blocks])
        DINV = sb("DINV", [P, z.blocks])
        MASK = sb("MASK", [P, z.blocks])
        FLAG = sb("FLAG", [P, 1], I32)
        IOTA = sb("IOTA", [P, P])
        PIDX = sb("PIDX", [P, 1])
        TRASH = sb("TRASH", [P, 1])
        IDENT = sb("IDENT", [P, P])
        LOWER = sb("LOWER", [P, P])
        ROW0 = sb("ROW0", [P, P])
        ONES = sb("ONES", [P, P])
        INT = sb("INT", [P, max(P, z.blocks)], I32)
        TINY = sb("TINY", [P, 8, NB_STEP])
        SMALL = sb("SMALL", [P, 4])
        STAT = sb("STAT", [P, 4, F])
        WK = sb("WK", [F, 25 * F])
        RFW = [sb(f"RFW{l}", [F + 1, 2 * F]) for l in range(2)]
        FW2 = sb("FW2", [F, F])
        MW1 = sb("MW1", [F + 1, 2 * HID])
        MWE = sb("MWE", [FEAT_E, HID])
        MW2 = sb("MW2", [HID, F])
        MB2 = sb("MB2", [P, F])
        UW1 = sb("UW1", [2 * F, HID])
        UB1 = sb("UB1", [HID, 1])
        UW2 = sb("UW2", [HID, F])
        UB2 = sb("UB2", [P, F])
        WDS = sb("WDS", [2 * F, 3, F])
        WE = sb("WE", [CAT_E, 3, F])
        GAM = sb("GAM", [P, 2, F])
        BET = sb("BET", [P, 2, F])
        G = sb("G", [P, CHUNKS, TILES // CHUNKS * CELL_W])
        OH = sb("OH", [P, CHUNKS, TILES // CHUNKS, P])
        IDX = sb("IDX", [P, CHUNKS, TILES // CHUNKS], I32)
        SIDX = sb("SIDX", [P, 1], I32)
        QIDX = sb("QIDX", [P, 1], I32)
        STG = sb("STG", [P, HID])
        STE = sb("STE", [P, CAT_E])
        EA = sb("EA", [P, CHUNKS, TILES // CHUNKS, CAT_E])
        EF = sb("EF", [FEAT_E, CHUNKS, TILES // CHUNKS * P])
        OHT = sb("OHT", [P, TILES // CHUNKS, P])
        QG = sb("QG", [P, HID])
        QW = sb("QW", [P, HID])
        ROWS = sb("ROWS", [P, P])
        HS = sb("HS", [P, CHUNKS, TILES // CHUNKS, HID])
        ST = sb("ST", [P, NB_STEP, P])
        HT = sb("HT", [P, NB_STEP * P])
        AG = sb("AG", [P, NB_STEP, HID])
        XC = sb("XC", [P, NB_STEP, F])
        SQ = sb("SQ", [P, NB_STEP, F])
        XW = sb("XW", [P, 2, 25 * F])
        TP = AG
        TQ = ST
        UT = sb("UT", [HID, NB_STEP * P])
        T17 = UT

        PS = ctx.enter_context(nc.psum_tensor("PS", [P, 8 * 512], F32))

        def bank(b, cols, rows=P):
            return PS[0:rows, b * 512:b * 512 + cols]

        WIN, WINE, ROW = bank(0, HID), bank(1, CAT_E), bank(6, P)
        OT = bank(2, TILES // CHUNKS * P)
        HIDP = bank(4, TILES // CHUNKS * P)
        psT = bank(0, NB_STEP * P)
        R0 = 3

        per_step = {"turned": (1, 2, 2, 1, 2, 2, 2, 2), "copied": (1, 2, 2, 1, 2, 2, 2, 2),
                    "stage0": (1, 1, 1, 1, 0, 1, 1, 1), "stage1": (0, 1, 1, 0, 1, 1, 1, 1),
                    "sums_in": (0,) + (16,) * 7, "sums_used": (0,) + (1,) * 7, "dve": (1,) * 8,
                    "var": (1, 0, 1, 1, 1), "rstd": (1, 0, 1, 1, 1)}

        def since(ph, what):
            return z.steps * sum(per_step[what][:int(ph[1:])])

        fast = Route("fast", z.groups, CHUNKS, TILES // CHUNKS, sem)
        slow = Route("slow", z.tiles, 1, 1, sem)
        pass_done = sem("pass_done")
        phase_done = sem("phase_done")
        flag_ready = sem("flag_ready")
        turn = sem("turn")

        block = ctx.enter_context(nc.Block())

        def per_route(eng, flag, run):
            with eng.If(flag):
                run(fast)
            with eng.Else():
                run(slow)

        def over_groups(eng, route, body):
            body(0, True)
            with eng.Fori(1, route.groups) as i:
                body(i, False)

        def free_cells(eng, ph, k, b):
            mine = (NB_STEP + 1) // 2 if b % 2 == 0 else NB_STEP // 2
            before = k * mine + b // 2
            if isinstance(before, int) and before == 0:
                return
            eng.wait_ge(sem(f"{ph}_cells_stored{b % 2}"), before * 8 * 16)

        def hold(eng):
            eng.sem_inc(turn, 1)

        def load_flag(eng):
            eng.wait_ge(flag_ready, 1)
            return eng.value_load(FLAG[0:1, 0:1], min_val=0, max_val=1)

        @block.sync
        def _(sp):
            loaded, zero_ready, zeroed = sem("loaded"), sem("zero_ready"), sem("zeroed")
            todo = [(REL[:, :].bitcast(I32), t["dst"]), (SLOTI[:, :], t["src"]),
                    (X[:, :, :].rearrange("p b f -> p (b f)")[:, 0:z.tiles * 2], t["ea2"]),
                    (WK[:, :], t["wk0"]), (FW2[:, :], t["fw"][2 * F:3 * F, :]),
                    (MW1[0:F, 0:HID], t["mw1"][0:F, :]), (MW1[0:F, HID:2 * HID], t["mw1"][F:2 * F, :]),
                    (MW1[F:F + 1, HID:2 * HID], t["mb1"]), (MWE[:, :], t["mw1"][2 * F:2 * F + FEAT_E, :]),
                    (MW2[:, :], t["mw2"]), (MB2[:, :], t["mb2"].to_broadcast([P, F])),
                    (UW1[:, :], t["uw1"]), (UB1[:, :], t["ub1"]), (UW2[:, :], t["uw2"]),
                    (UB2[:, :], t["ub2"].to_broadcast([P, F])),
                    (RFW[0][F:F + 1, F:2 * F], t["fb"])]
            for l in range(2):
                todo += [(RFW[l][0:F, 0:F], t["roots"][l]), (RFW[l][F:F + 1, 0:F], t["biases"][l:l + 1, :]),
                         (RFW[l][0:F, F:2 * F], t["fw"][l * F:(l + 1) * F, :]),
                         (GAM[:, l, :], t[f"g{l}"].to_broadcast([P, F])),
                         (BET[:, l, :], t[f"be{l}"].to_broadcast([P, F]))]
            for l in range(3):
                todo += [(WDS[:, l, :], t[f"w{l}"][0:2 * F, :]), (WE[0:16, l, :], t[f"w{l}"][2 * F:2 * F + 16, :]),
                         (WE[16:17, l, :], t[f"b{l}"])]
            sp.wait_ge(sem("weights_zeroed"), 2)
            hold(sp)
            for dst, src in todo:
                sp.dma_start(dst, src).then_inc(loaded, 16)
            sem_loaded_total[0] = 16 * len(todo)
            sp.wait_ge(zero_ready, 1)
            hold(sp)
            n = 0
            for acc, width in [(p[3], p[3].shape[1]) for p in passes] + [(acc_ea, CAT_E)]:
                rows = acc.rearrange("(k p b) c -> p k (b c)", p=P, b=NB_STEP)
                with sp.Fori(0, z.steps) as k:
                    sp.dma_start(rows[:, bass.ds(k, 1), :].rearrange("p k c -> p (k c)"),
                                 AG[:, :, :].rearrange("p b c -> p (b c)")[:, 0:NB_STEP * width]).then_inc(zeroed, 16)
                n += z.steps
            sp.wait_ge(sem("cell_ready"), 1)
            hold(sp)
            sp.dma_start(cell_idx, SLOTF[:, :].bitcast(I32)).then_inc(sem("cell_stored"), 16)
            sp.wait_ge(sem("edges_ready"), 1)
            hold(sp)
            sp.dma_start(X[:, :, :], t["x"].rearrange("(b p) f -> p b f", p=P)).then_inc(sem("x_in"), 16)
            sp.wait_ge(zeroed, 16 * n)
            hold(sp)
            sp.wait_ge(sem("cell_stored"), 16)
            hold(sp)
            flag = load_flag(sp)

            def store_cells(ph, k, first):
                for b in range(NB_STEP):
                    sp.wait_ge(sem(f"{ph}_xw_act"), k * 3 * NB_STEP + 3 * (b + 1))
                    hold(sp)
                    sp.wait_ge(sem(f"{ph}_xw_dve"), k * 2 * NB_STEP + 2 * (b + 1))
                    hold(sp)
                    rows = t_cell.rearrange("(n p v u) c -> n p v u c", p=P, v=4, u=4)
                    to = rows[bass.ds(k * NB_STEP + b, 1)].rearrange("n p v u c -> (n p) v u c")
                    w = XW[:, b % 2, :].rearrange("p (v u f) -> p v u f", v=5, u=5)
                    for bit in range(2):
                        for v in range(4):
                            src = XW[:, b % 2, (v + bit) * 5 * F:(v + bit + 1) * 5 * F]
                            pairs = bass.AP(src.tensor, src.offset, [src.ap[0], [F, 4], [1, 2 * F]])
                            sp.dma_start(to[:, v, :, bit * 2 * F:(bit + 1) * 2 * F], pairs
                                         ).then_inc(sem(f"{ph}_cells_stored{b % 2}"), 16)

            def end_phase(ph, stores, dve_steps):
                for s, v in stores:
                    sp.wait_ge(s, v)
                    hold(sp)
                sp.wait_ge(sem("dve"), since(ph, "dve") + dve_steps)
                hold(sp)
                sp.sem_inc(phase_done, 1)

            even, odd = (NB_STEP + 1) // 2 * 8 * 16, NB_STEP // 2 * 8 * 16

            def load_sums(ph, acc, k, first):
                if not first:
                    sp.wait_ge(sem("sums_used"), since(ph, "sums_used") + k)
                    hold(sp)
                width = acc.shape[1]
                rows = acc.rearrange("(b p) c -> p b c", p=P)
                sp.dma_start(AG[:, :, 0:width] if width < HID else AG[:, :, :],
                             rows[:, bass.ds(k * NB_STEP, NB_STEP), :]).then_inc(sem("sums_in"), 16)

            def over_steps(body):
                body(0, True)
                with sp.Fori(1, z.steps) as k:
                    body(k, False)

            def run_pass(n):
                kind, table, width, acc = passes[n]

                def run(r):
                    base = r.groups * n

                    def body(i, first):
                        for c in range(r.chunks):
                            at = i * (r.chunks * r.chunk_tiles) + c * r.chunk_tiles
                            if not first:
                                sp.wait_ge(r.gathered[c], 16 * r.chunk_tiles * (base + i))
                                hold(sp)
                            src = cell_idx if kind == "spline" else t["src"]
                            sp.dma_start(IDX[:, c, 0:r.chunk_tiles], src[:, bass.ds(at, r.chunk_tiles)]
                                         ).then_inc(r.idx_in[c], 16)
                            if n == 0 or kind == "mlp":
                                if not first:
                                    sp.wait_ge(r.chunk_done, r.chunks * (base + i - 1) + c + 1)
                                    hold(sp)
                            if n == 0:
                                sp.dma_start(EA[:, c, 0:r.chunk_tiles, :],
                                             t["ea17"][:, bass.ds(at, r.chunk_tiles), :]).then_inc(r.ea_in[c], 16)
                            if kind == "mlp":
                                sp.dma_start(EF[:, c, 0:r.chunk_tiles * P],
                                             t["ef"][:, bass.ds(at * P, r.chunk_tiles * P)]).then_inc(r.ef_in[c], 16)
                                if c == 0:
                                    if not first:
                                        sp.wait_ge(r.q_in, 16 * i)
                                        hold(sp)
                                    sp.dma_start(QIDX[:, :], SLOTI[:, bass.ds(i, 1)]).then_inc(r.qidx_in, 16)
                    over_groups(sp, r, body)
                per_route(sp, flag, run)

            over_steps(lambda k, first: store_cells("n0", k, first))
            end_phase("n0", [(sem("n0_cells_stored0"), z.steps * even), (sem("n0_cells_stored1"), z.steps * odd)],
                      z.steps)
            sp.wait_ge(phase_done, 1)
            hold(sp)
            run_pass(0)
            sp.wait_ge(pass_done, 1)
            hold(sp)
            sp.dma_start(WK[:, :], t["wk1"]).then_inc(sem("wk1_in"), 16)
            sp.dma_start(S17[:, :, :], acc_ea.rearrange("(b p) c -> p b c", p=P)).then_inc(sem("s17_in"), 16)

            def n1(k, first):
                load_sums("n1", passes[0][3], k, first)
                store_cells("n1", k, first)
            over_steps(n1)
            end_phase("n1", [(sem("n1_cells_stored0"), z.steps * even), (sem("n1_cells_stored1"), z.steps * odd)],
                      z.steps)
            run_pass(1)
            sp.wait_ge(pass_done, 2)
            hold(sp)

            def store_rows(ph, table, k, stage, what):
                sp.wait_ge(sem(f"{ph}_{what}_ready"), k + 1)
                hold(sp)
                sp.dma_start(table.rearrange("(b p) c -> p b c", p=P)[:, bass.ds(k * NB_STEP, NB_STEP), :],
                             stage).then_inc(sem(f"{ph}_{what}_stored"), 16)

            def n2(k, first):
                load_sums("n2", passes[1][3], k, first)
                store_rows("n2", t_gcn, k, SQ[:, :, :], "rows")
            over_steps(n2)
            end_phase("n2", [(sem("n2_rows_stored"), 16 * z.steps)], z.steps)
            run_pass(2)
            sp.wait_ge(pass_done, 3)
            hold(sp)

            def n3(k, first):
                if not first:
                    sp.wait_ge(sem("n3_p_stored"), 16 * k)
                    hold(sp)
                load_sums("n3", passes[2][3], k, first)
                store_rows("n3", t_p, k, TP[:, :, :], "p")
                store_rows("n3", t_q, k, TQ[:, :, :], "q")
            over_steps(n3)
            end_phase("n3", [(sem("n3_p_stored"), 16 * z.steps), (sem("n3_q_stored"), 16 * z.steps)], z.steps)
            run_pass(3)
            sp.wait_ge(pass_done, 4)
            hold(sp)
            over_steps(lambda k, first: load_sums("n4", passes[3][3], k, first))
            sp.wait_ge(sem("dve"), since("n4", "dve") + z.steps)
            hold(sp)
            sp.dma_start(t_mp[0].rearrange("(b p) c -> p b c", p=P), H[:, :, :]).then_inc(sem("mp0_stored"), 16)
            end_phase("n4", [(sem("mp0_stored"), 16)], z.steps)
            for l in range(3):
                run_pass(4 + l)
                sp.wait_ge(pass_done, 5 + l)
                hold(sp)
                ph = f"n{5 + l}"
                over_steps(lambda k, first: load_sums(ph, passes[4 + l][3], k, first))
                if l < 2:
                    sp.wait_ge(sem(f"{ph}_normed"), 1)
                    hold(sp)
                    sp.dma_start(t_mp[l + 1].rearrange("(b p) c -> p b c", p=P), H[:, :, :]
                                 ).then_inc(sem(f"mp{l + 1}_stored"), 16)
                    end_phase(ph, [(sem(f"mp{l + 1}_stored"), 16)], z.steps)
            sp.wait_ge(sem("dve"), since("n7", "dve") + z.steps)
            hold(sp)
            sp.dma_start(t["out"].rearrange("(b p) f -> p b f", p=P), X[:, :, :]).then_inc(sem("out_stored"), 16)
            sp.wait_ge(sem("out_stored"), 16)
            hold(sp)

        @block.gpsimd
        def _(pool):
            ints = sem("ints")
            nc.gpsimd.iota(INT[:, 0:P], pattern=[[1, P]], base=0, channel_multiplier=0).then_inc(ints, 1)
            pool.wait_ge(ints, 1)
            nc.gpsimd.tensor_copy(IOTA[:, :], INT[:, 0:P]).then_inc(ints, 1)
            pool.wait_ge(ints, 2)
            nc.gpsimd.iota(INT[:, 0:z.blocks], pattern=[[P, z.blocks]], base=0, channel_multiplier=1).then_inc(ints, 1)
            pool.wait_ge(ints, 3)
            nc.gpsimd.tensor_copy(MASK[:, :], INT[:, 0:z.blocks]).then_inc(sem("iota_ready"), 1)
            flag = load_flag(pool)

            def run_pass(n):
                kind, table, width, acc = passes[n]

                def run(r):
                    base = r.groups * n
                    ct = r.chunk_tiles

                    def scatter(j):
                        pool.wait_ge(r.win_staged, base + j + 1)
                        pool.wait_ge(r.slots_staged, base + j + 1)
                        if n == 0:
                            pool.wait_ge(r.ea_staged, j + 1)
                        hold(pool)
                        to = bass.IndirectOffsetOnAxis(ap=SIDX[:, 0:1], axis=0)
                        nc.gpsimd.indirect_dma_start(acc, to, STG[:, 0:acc.shape[1]], None,
                                                     compute_op=ALU.add).then_inc(r.scattered, 16)
                        if n == 0:
                            nc.gpsimd.indirect_dma_start(acc_ea, to, STE[:, :], None,
                                                         compute_op=ALU.add).then_inc(r.ea_scattered, 16)

                    def body(i, first):
                        if kind == "mlp":
                            pool.wait_ge(r.qidx_in, 16 * (i + 1))
                            if not first:
                                pool.wait_ge(r.q_copied, i)
                            hold(pool)
                            nc.gpsimd.indirect_dma_start(QG[:, :], None, t_q, bass.IndirectOffsetOnAxis(
                                ap=QIDX[:, 0:1], axis=0)).then_inc(r.q_in, 16)
                        for c in range(r.chunks):
                            pool.wait_ge(r.idx_in[c], 16 * (base + i + 1))
                            if not first:
                                pool.wait_ge(r.chunk_done, r.chunks * (base + i - 1) + c + 1)
                            hold(pool)
                            for j in range(ct):
                                nc.gpsimd.indirect_dma_start(
                                    G[:, c, j * width:(j + 1) * width], None, table,
                                    bass.IndirectOffsetOnAxis(ap=IDX[:, c, j:j + 1], axis=0)
                                ).then_inc(r.gathered[c], 16)
                            if not first and c == min(1, r.chunks - 1):
                                scatter(i - 1)
                    over_groups(pool, r, body)
                    scatter(r.groups - 1)
                    pool.wait_ge(r.scattered, 16 * (base + r.groups))
                    if n == 0:
                        pool.wait_ge(r.ea_scattered, 16 * r.groups)
                    pool.sem_inc(pass_done, 1)
                per_route(pool, flag, run)

            for n in range(len(passes)):
                pool.wait_ge(phase_done, n + 1)
                run_pass(n)

        @block.tensor
        def _(pe):
            pe.wait_ge(sem("dst_ready"), 1)
            nc.tensor.matmul(bank(7, z.groups), ROW0[:, :],
                             DSTF[:, :].rearrange("p (g j) -> p g j", j=TILES)[:, :, 0],
                             start=True, stop=True).then_inc(sem("base_ps"), 1)
            pe.wait_ge(sem("misfits_ready"), 1)
            nc.tensor.matmul(bank(7, 1), ONES[:, :], SMALL[:, 0:1], start=True, stop=True
                             ).then_inc(sem("misfits_ps"), 1)
            flag = load_flag(pe)

            def turn(ph, k, r, rounds, src, cols, rows=P):
                pe.wait_ge(sem(f"stage{r}"), since(ph, f"stage{r}") + k + 1)
                hold(pe)
                for b in range(NB_STEP):
                    last = nc.tensor.transpose(psT[0:cols, b * P:(b + 1) * P], src[:, b, 0:cols], IDENT[:, :])
                last.then_inc(sem("turned"), 1)
                pe.wait_ge(sem("copied"), since(ph, "copied") + rounds * k + r + 1)

            def cells(ph, k, first):
                for b in range(NB_STEP):
                    for v in range(5):
                        if not (first and b == 0):
                            if v % 2 == 0:
                                pe.wait_ge(sem(f"{ph}_xw_act"), k * 3 * NB_STEP + 3 * (b - 1) + v // 2 + 1)
                            else:
                                pe.wait_ge(sem(f"{ph}_xw_dve"), k * 2 * NB_STEP + 2 * (b - 1) + v // 2 + 1)
                        nc.tensor.matmul(bank(R0 + v, 5 * F), HT[0:F, b * P:(b + 1) * P],
                                         WK[:, v * 5 * F:(v + 1) * 5 * F], start=True, stop=True
                                         ).then_inc(sem(f"{ph}_xw_ps"), 1)

            def products(ph, k, what, lhs, rhs, width, per_bank, at=R0):
                for b in range(NB_STEP):
                    col = (at + b // per_bank) * 512 + b % per_bank * width
                    for n, (lh, rh) in enumerate(zip(lhs, rhs)):
                        last = nc.tensor.matmul(PS[:, col:col + width], lh[:, b * P:(b + 1) * P], rh,
                                                start=(n == 0), stop=(n == len(lhs) - 1))
                last.then_inc(sem(f"{ph}_{what}"), 1)

            def over_steps(body):
                body(0, True)
                with pe.Fori(1, z.steps) as k:
                    body(k, False)

            def run_pass(n):
                kind, table, width, acc = passes[n]
                out_w = acc.shape[1]

                def run(r):
                    base = r.groups * n
                    ct = r.chunk_tiles

                    def body(i, first):
                        for c in range(r.chunks):
                            if not r.fast:
                                pe.wait_ge(r.row_staged, base + i + 1)
                                nc.tensor.matmul(ROW, ROWS[:, :], IDENT[:, :], start=True, stop=True
                                                 ).then_inc(r.row_ready, 1)
                            pe.wait_ge(r.oh_ready, r.chunks * (base + i) + c + 1)
                            if kind == "mlp":
                                for j in range(ct):
                                    last = nc.tensor.transpose(OT[:, j * P:(j + 1) * P], OH[:, c, j, :], IDENT[:, :])
                                last.then_inc(r.oh_turned, 1)
                                pe.wait_ge(r.ef_in[c], 16 * (i + 1))
                                if c == 0:
                                    pe.wait_ge(r.q_copied, i + 1)
                                pe.wait_ge(r.oht_ready, r.chunks * i + c + 1)
                                for j in range(ct):
                                    nc.tensor.matmul(HIDP[:, j * HID:(j + 1) * HID], EF[:, c, j * P:(j + 1) * P],
                                                     MWE[:, :], start=True, stop=False)
                                    last = nc.tensor.matmul(HIDP[:, j * HID:(j + 1) * HID], OHT[:, j, :],
                                                            QW[:, :], start=False, stop=True)
                                last.then_inc(r.hid_done, 1)
                                pe.wait_ge(r.hid_ready, r.chunks * i + c + 1)
                            elif kind == "spline":
                                pe.wait_ge(r.prod_ready, r.chunks * (r.groups * n + i) + c + 1)
                            else:
                                pe.wait_ge(r.gathered[c], 16 * ct * (base + i + 1))
                            if n == 0:
                                pe.wait_ge(r.ea_in[c], 16 * (i + 1))
                            if c == 0 and not first:
                                pe.wait_ge(r.win_staged, base + i)
                                if n == 0:
                                    pe.wait_ge(r.ea_staged, i)
                            if n == 0:
                                for j in range(ct):
                                    nc.tensor.matmul(WINE, OH[:, c, j, :], EA[:, c, j, :],
                                                     start=(c == 0 and j == 0), stop=(c == r.chunks - 1 and j == ct - 1))
                            parts = 4 if kind == "spline" else 1
                            for j in range(ct):
                                for s in range(parts):
                                    rhs = (HS[:, c, j, :] if kind == "mlp"
                                           else G[:, c, j * width + s * F:j * width + (s + 1) * F])
                                    last = nc.tensor.matmul(
                                        WIN[:, 0:out_w], OH[:, c, j, :], rhs, start=(c == 0 and j == 0 and s == 0),
                                        stop=(c == r.chunks - 1 and j == ct - 1 and s == parts - 1))
                            last.then_inc(r.chunk_done, 1)
                    if n == 0 and not r.fast:
                        with pe.Fori(0, z.tiles) as i:
                            pe.wait_ge(sem("tile_staged"), i + 1)
                            nc.tensor.matmul(ROW, ROWS[:, :], IDENT[:, :], start=True, stop=True
                                             ).then_inc(sem("tile_row"), 1)
                    over_groups(pe, r, body)
                per_route(pe, flag, run)

            def n0(k, first):
                turn("n0", k, 0, 1, ST, F)
                cells("n0", k, first)
            over_steps(n0)
            pe.wait_ge(phase_done, 1)
            run_pass(0)
            pe.wait_ge(pass_done, 1)
            pe.wait_ge(sem("wk1_in"), 16)

            def n1(k, first):
                turn("n1", k, 0, 2, ST, F)
                if not first:
                    pe.wait_ge(sem("n1_xw_act"), k * 3 * NB_STEP)
                    pe.wait_ge(sem("n1_xw_dve"), k * 2 * NB_STEP)
                products("n1", k, "rf_ps", [HT[0:F + 1, :]], [RFW[0][:, :]], 2 * F, 4)
                turn("n1", k, 1, 2, ST, F)
                cells("n1", k, first)
            over_steps(n1)
            pe.wait_ge(phase_done, 2)
            run_pass(1)
            pe.wait_ge(pass_done, 2)

            def n2(k, first):
                turn("n2", k, 0, 2, ST, F)
                products("n2", k, "rf_ps", [HT[0:F + 1, :]], [RFW[1][:, :]], 2 * F, 4)
                turn("n2", k, 1, 2, ST, F)
                products("n2", k, "f_ps", [HT[0:F, :]], [FW2[:, :]], F, 8, 6)
            over_steps(n2)
            pe.wait_ge(phase_done, 3)
            run_pass(2)
            pe.wait_ge(pass_done, 3)

            def n3(k, first):
                turn("n3", k, 0, 1, ST, F)
                products("n3", k, "pq_ps", [HT[0:F + 1, :]], [MW1[:, :]], 2 * HID, 2)
            over_steps(n3)
            pe.wait_ge(phase_done, 4)
            run_pass(3)
            pe.wait_ge(pass_done, 4)

            def n4(k, first):
                pe.wait_ge(sem("sums_in"), since("n4", "sums_in") + 16 * (k + 1))
                for b in range(NB_STEP):
                    last = nc.tensor.transpose(psT[:, b * P:(b + 1) * P], AG[:, b, :], IDENT[:, :])
                last.then_inc(sem("turned"), 1)
                pe.wait_ge(sem("copied"), since("n4", "copied") + 2 * k + 1)
                products("n4", k, "agg_ps", [HT[:, :]], [MW2[:, :]], F, 8)
                turn("n4", k, 1, 2, ST, P)
                for j in range(NB_STEP // 3):
                    last = nc.tensor.matmul(bank(R0 + j, 3 * P), UW1[:, :], HT[:, j * 3 * P:(j + 1) * 3 * P],
                                            start=True, stop=True)
                last.then_inc(sem("n4_u_ps"), 1)
                pe.wait_ge(sem("n4_u_ready"), k + 1)
                products("n4", k, "y_ps", [UT[:, :]], [UW2[:, :]], F, 8, 6)
            over_steps(n4)
            for l in range(3):
                pe.wait_ge(phase_done, 5 + l)
                run_pass(4 + l)
                pe.wait_ge(pass_done, 5 + l)
                ph = f"n{5 + l}"

                def n5(k, first):
                    turn(ph, k, 0, 2, ST, P)
                    turn(ph, k, 1, 2, XC, CAT_E)
                    products(ph, k, "m_ps", [HT[:, :], T17[0:CAT_E, :]], [WDS[:, l, :], WE[:, l, :]], F, 8)
                over_steps(n5)
                if l < 2:
                    for s in range(2):
                        pe.wait_ge(sem(f"{ph}_colsum"), s + 1)
                        nc.tensor.matmul(bank(7, F), ONES[:, :], STAT[:, 0, :], start=True, stop=True
                                         ).then_inc(sem(f"{ph}_total"), 1)

        @block.scalar
        def _(act):
            copy = ACT.Copy

            def turned(ph, k, r, rounds, rows, to=HT):
                act.wait_ge(sem("turned"), since(ph, "turned") + rounds * k + r + 1)
                nc.scalar.activation(to[0:rows, :], psT[0:rows, :], copy).then_inc(sem("copied"), 1)

            def root(ph, k):
                act.wait_ge(sem("var"), since(ph, "var") + k + 1)
                nc.scalar.activation(TINY[:, 3, :], TINY[:, 2, :], ACT.Sqrt).then_inc(sem("rstd"), 1)

            def cells(ph, k):
                for b in range(NB_STEP):
                    for v in range(0, 5, 2):
                        act.wait_ge(sem(f"{ph}_xw_ps"), k * 5 * NB_STEP + 5 * b + v + 1)
                        free_cells(act, ph, k, b)
                        nc.scalar.activation(XW[:, b % 2, v * 5 * F:(v + 1) * 5 * F], bank(R0 + v, 5 * F), copy
                                             ).then_inc(sem(f"{ph}_xw_act"), 1)

            def over_steps(body):
                body(0, True)
                with act.Fori(1, z.steps) as k:
                    body(k, False)

            def run_pass(n):
                kind, table, width, acc = passes[n]
                out_w = acc.shape[1]

                def run(r):
                    base = r.groups * n

                    def body(i, first):
                        if kind == "mlp":
                            act.wait_ge(r.q_in, 16 * (i + 1))
                            if not first:
                                act.wait_ge(r.hid_done, r.chunks * i)
                            nc.scalar.activation(QW[:, :], QG[:, :], copy).then_inc(r.q_copied, 1)
                            for c in range(r.chunks):
                                act.wait_ge(r.oh_turned, r.chunks * i + c + 1)
                                nc.scalar.activation(OHT[:, 0:r.chunk_tiles, :],
                                                     OT.rearrange("p (j e) -> p j e", e=P)[:, 0:r.chunk_tiles, :],
                                                     copy).then_inc(r.oht_ready, 1)
                                act.wait_ge(r.hid_added, r.chunks * i + c + 1)
                                nc.scalar.activation(HS[:, c, 0:r.chunk_tiles, :], HS[:, c, 0:r.chunk_tiles, :],
                                                     ACT.Relu).then_inc(r.hid_ready, 1)
                        act.wait_ge(r.chunk_done, r.chunks * (base + i + 1))
                        if not first:
                            act.wait_ge(r.scattered, 16 * (base + i))
                            if n == 0:
                                act.wait_ge(r.ea_scattered, 16 * i)
                        if n == 0:
                            nc.scalar.activation(STE[:, :], WINE, copy).then_inc(r.ea_staged, 1)
                        nc.scalar.activation(STG[:, 0:out_w], WIN[:, 0:out_w], copy).then_inc(r.win_staged, 1)
                        nc.scalar.activation(SIDX[:, :], SLOTI[:, bass.ds(i, 1)], copy).then_inc(r.slots_staged, 1)
                    over_groups(act, r, body)
                per_route(act, flag, run)

            flag = load_flag(act)

            def n0(k, first):
                root("n0", k)
                turned("n0", k, 0, 1, F)
                cells("n0", k)
            over_steps(n0)
            act.wait_ge(phase_done, 1)
            run_pass(0)
            act.wait_ge(pass_done, 1)
            act.wait_ge(sem("invdeg_ready"), 1)
            nc.scalar.activation(DINV[:, :], INVD[:, :], ACT.Sqrt).then_inc(sem("invroot_ready"), 1)

            def n1(k, first):
                turned("n1", k, 0, 2, F)
                turned("n1", k, 1, 2, F)
                cells("n1", k)
            over_steps(n1)
            act.wait_ge(phase_done, 2)
            run_pass(1)
            act.wait_ge(pass_done, 2)

            def n2(k, first):
                turned("n2", k, 0, 2, F)
                turned("n2", k, 1, 2, F)
                root("n2", k)
            over_steps(n2)
            act.wait_ge(phase_done, 3)
            run_pass(2)
            act.wait_ge(pass_done, 3)

            def n3(k, first):
                root("n3", k)
                turned("n3", k, 0, 1, F)
                act.wait_ge(sem("n3_pq_ps"), k + 1)
                for j in range(-(-NB_STEP // 2)):
                    m = min(2, NB_STEP - 2 * j)
                    src = bank(R0 + j, m * 2 * HID).rearrange("p (b w) -> p b w", w=2 * HID)
                    last = nc.scalar.activation(TP[:, 2 * j:2 * j + m, :], src[:, :, 0:HID], copy)
                last.then_inc(sem("n3_p_ready"), 1)
                for j in range(-(-NB_STEP // 2)):
                    m = min(2, NB_STEP - 2 * j)
                    src = bank(R0 + j, m * 2 * HID).rearrange("p (b w) -> p b w", w=2 * HID)
                    last = nc.scalar.activation(TQ[:, 2 * j:2 * j + m, :], src[:, :, HID:2 * HID], copy)
                last.then_inc(sem("n3_q_ready"), 1)
            over_steps(n3)
            act.wait_ge(phase_done, 4)
            run_pass(3)
            act.wait_ge(pass_done, 4)

            def n4(k, first):
                turned("n4", k, 0, 2, P)
                turned("n4", k, 1, 2, P)
                act.wait_ge(sem("n4_u_ps"), k + 1)
                for j in range(NB_STEP // 3):
                    last = nc.scalar.activation(UT[:, j * 3 * P:(j + 1) * 3 * P], bank(R0 + j, 3 * P), ACT.Relu,
                                                bias=UB1[:, 0:1])
                last.then_inc(sem("n4_u_ready"), 1)
                root("n4", k)
            over_steps(n4)
            for l in range(3):
                act.wait_ge(phase_done, 5 + l)
                run_pass(4 + l)
                act.wait_ge(pass_done, 5 + l)
                ph = f"n{5 + l}"

                def n5(k, first):
                    turned(ph, k, 0, 2, P)
                    turned(ph, k, 1, 2, CAT_E, T17)
                over_steps(n5)
                if l < 2:
                    act.wait_ge(sem(f"bn{l}_var"), 1)
                    nc.scalar.activation(STAT[:, 3, :], STAT[:, 2, :], ACT.Sqrt).then_inc(sem(f"bn{l}_rstd"), 1)

        @block.vector
        def _(dve):
            v = nc.vector
            setup = sem("setup_dve")
            count = [0]

            def link(instruction):
                count[0] += 1
                instruction.then_inc(setup, 1)
                dve.wait_ge(setup, count[0])

            def bc(ap, shape):
                return ap.unsqueeze(2).to_broadcast(shape)

            v.memset(MW1[F:F + 1, 0:HID], 0.0).then_inc(sem("weights_zeroed"), 1)
            v.memset(RFW[1][F:F + 1, F:2 * F], 0.0).then_inc(sem("weights_zeroed"), 1)
            link(v.memset(ONES[:, :], 1.0))
            link(v.memset(HT[F:F + 1, :], 1.0))
            v.memset(AG[:, :, :], 0.0).then_inc(sem("zero_ready"), 1)
            dve.wait_ge(sem("iota_ready"), 1)
            link(v.tensor_copy(PIDX[:, :], MASK[:, 0:1]))
            link(v.tensor_scalar(TRASH[:, :], PIDX[:, :], float(z.nodes + 1), None, ALU.add))
            link(v.tensor_scalar(MASK[:, :], MASK[:, :], float(z.nodes), None, ALU.is_lt))
            link(v.tensor_scalar(IDENT[:, :], IOTA[:, :], PIDX[:, 0:1], None, ALU.is_equal))
            link(v.tensor_scalar(LOWER[:, :], IOTA[:, :], PIDX[:, 0:1], None, ALU.is_lt))
            link(v.tensor_scalar(ROW0[:, :], ONES[:, :], IDENT[:, 0:1], None, ALU.mult))
            dve.wait_ge(sem("loaded"), sem_loaded_total[0])
            link(v.tensor_copy(DSTF[:, :], REL[:, :].bitcast(I32)))
            v.tensor_copy(SMALL[:, 3:4], DSTF[:, 0:1]).then_inc(sem("dst_ready"), 1)
            dve.wait_ge(sem("base_ps"), 1)
            base = STAT[:, 0:4, :].rearrange("p a f -> p (a f)")[:, 0:z.groups]
            link(v.tensor_copy(base, bank(7, z.groups)))
            in_groups = "p (g j) -> p g j"
            link(v.tensor_tensor(REL[:, :].rearrange(in_groups, j=TILES), DSTF[:, :].rearrange(in_groups, j=TILES),
                                 bc(base, [P, z.groups, TILES]), ALU.subtract))
            flat = COEF[:, 0:z.tiles]
            link(v.tensor_scalar(flat, REL[:, :], 0.0, None, ALU.is_lt))
            link(v.tensor_reduce(SMALL[:, 1:2], flat, AX.X, ALU.add))
            link(v.tensor_scalar(flat, REL[:, :], float(P), None, ALU.is_ge))
            link(v.tensor_reduce(SMALL[:, 2:3], flat, AX.X, ALU.add))
            v.tensor_tensor(SMALL[:, 0:1], SMALL[:, 1:2], SMALL[:, 2:3], ALU.add).then_inc(sem("misfits_ready"), 1)
            ev = X[:, :, :].rearrange("p b f -> p (b f)")[:, 0:z.tiles * 2]
            fl = H[:, :, :].rearrange("p b f -> p (b f)")[:, 0:z.tiles * 2]
            link(v.tensor_scalar(ev, ev, 4.0, 0.0, ALU.mult, ALU.max))
            link(v.tensor_scalar(ev, ev, 4.0, None, ALU.min))
            link(v.tensor_scalar(fl, ev, 1.0, None, ALU.is_ge))
            for edge in (2.0, 3.0):
                link(v.scalar_tensor_tensor(out=fl, in0=ev, scalar=edge, in1=fl, op0=ALU.is_ge, op1=ALU.add))
            link(v.tensor_tensor(ev, ev, fl, ALU.subtract))
            f2 = fl.rearrange("p (t d) -> p t d", d=2)
            e2 = ev.rearrange("p (t d) -> p t d", d=2)
            link(v.scalar_tensor_tensor(out=flat, in0=f2[:, :, 1], scalar=4.0, in1=f2[:, :, 0],
                                        op0=ALU.mult, op1=ALU.add))
            link(v.tensor_copy(SLOTF[:, :], SLOTI[:, :]))
            link(v.scalar_tensor_tensor(out=flat, in0=SLOTF[:, :], scalar=float(CELLS), in1=flat,
                                        op0=ALU.mult, op1=ALU.add))
            link(v.tensor_copy(SLOTF[:, :].bitcast(I32), flat))
            link(v.tensor_scalar(fl, ev, -1.0, 1.0, ALU.mult, ALU.add))
            v.tensor_copy(SMALL[:, 3:4], PIDX[:, :]).then_inc(sem("cell_ready"), 1)
            for s, (a, b) in enumerate([(f2, f2), (e2, f2), (f2, e2), (e2, e2)]):
                link(v.tensor_tensor(coef[:, :, s], a[:, :, 0], b[:, :, 1], ALU.mult))
            v.tensor_copy(SMALL[:, 3:4], PIDX[:, :]).then_inc(sem("edges_ready"), 1)
            link(v.tensor_scalar(base, base, PIDX[:, 0:1], None, ALU.add))
            link(v.tensor_copy(SLOTI[:, 0:z.groups], base))
            dve.wait_ge(sem("misfits_ps"), 1)
            link(v.tensor_scalar(SMALL[:, 0:1], bank(7, 1), 0.5, None, ALU.is_lt))
            v.tensor_copy(FLAG[:, :], SMALL[:, 0:1]).then_inc(flag_ready, 1)
            dve.wait_ge(sem("x_in"), 16)
            flag = load_flag(dve)

            NF = [P, NB_STEP, F]

            def over_steps(body):
                body(0, True)
                with dve.Fori(1, z.steps) as k:
                    body(k, False)

            def part(a, k):
                return a[:, bass.ds(k * NB_STEP, NB_STEP)]

            def norm(ph, k, link):
                x = part(X, k)
                hold(dve)
                link(v.tensor_reduce(TINY[:, 0, :], x, AX.X, ALU.add))
                link(v.tensor_scalar(TINY[:, 0, :], TINY[:, 0, :], 1.0 / F, None, ALU.mult))
                link(v.tensor_tensor(XC[:, :, :], x, bc(TINY[:, 0, :], NF), ALU.subtract))
                link(v.tensor_tensor(SQ[:, :, :], XC[:, :, :], XC[:, :, :], ALU.mult))
                link(v.tensor_reduce(TINY[:, 1, :], SQ[:, :, :], AX.X, ALU.add))
                link(v.tensor_scalar(TINY[:, 1, :], TINY[:, 1, :], 1.0 / F, EPS, ALU.mult, ALU.add))
                v.reciprocal(TINY[:, 2, :], TINY[:, 1, :]).then_inc(sem("var"), 1)
                dve.wait_ge(sem("rstd"), since(ph, "rstd") + k + 1)
                link(v.tensor_scalar(XC[:, :, :], XC[:, :, :], 0.0, None, ALU.max))
                link(v.tensor_tensor(part(H, k), XC[:, :, :], bc(TINY[:, 3, :], NF), ALU.mult))

            def cells(ph, k):
                for b in range(NB_STEP):
                    for q in range(1, 5, 2):
                        dve.wait_ge(sem(f"{ph}_xw_ps"), k * 5 * NB_STEP + 5 * b + q + 1)
                        free_cells(dve, ph, k, b)
                        v.tensor_copy(XW[:, b % 2, q * 5 * F:(q + 1) * 5 * F], bank(R0 + q, 5 * F)
                                      ).then_inc(sem(f"{ph}_xw_dve"), 1)

            def stage(ph, k, r, src, to=None):
                hold(dve)
                v.tensor_copy(ST[:, :, 0:F] if to is None else to, src).then_inc(sem(f"stage{r}"), 1)

            def finish(ph):
                v.tensor_copy(SMALL[:, 3:4], PIDX[:, :]).then_inc(sem("dve"), 1)

            def run_pass(n):
                kind, table, width, acc = passes[n]

                def run(r):
                    base = r.groups * n
                    ct = r.chunk_tiles

                    def body(i, first):
                        for c in range(r.chunks):
                            at = i * (r.chunks * ct) + c * ct
                            shape = [P, ct, P]
                            if not first:
                                dve.wait_ge(r.chunk_done, r.chunks * (base + i - 1) + c + 1)
                            if r.fast:
                                of, slots = REL, IOTA[:, :]
                            else:
                                hold(dve)
                                v.tensor_copy(ROWS[:, :], SLOTF[:, bass.ds(i, 1)].to_broadcast([P, P])
                                              ).then_inc(r.row_staged, 1)
                                dve.wait_ge(r.row_ready, base + i + 1)
                                of, slots = DSTF, ROW
                            v.tensor_tensor(OH[:, c, 0:ct, :], bc(of[:, bass.ds(at, ct)], shape),
                                            slots.unsqueeze(1).to_broadcast(shape), ALU.is_equal).then_inc(r.oh_ready, 1)
                            if kind == "spline":
                                dve.wait_ge(r.gathered[c], 16 * ct * (base + i + 1))
                                g = G[:, c, 0:ct * CELL_W].rearrange("p (a f) -> p a f", f=F)
                                w = COEF[:, bass.ds(at * 4, ct * 4)]
                                v.tensor_tensor(g, g, bc(w, [P, ct * 4, F]), ALU.mult).then_inc(r.prod_ready, 1)
                            if kind == "mlp":
                                dve.wait_ge(r.gathered[c], 16 * ct * (base + i + 1))
                                dve.wait_ge(r.hid_done, r.chunks * i + c + 1)
                                v.tensor_tensor(HS[:, c, 0:ct, :].rearrange("p j h -> p (j h)"), HIDP[:, 0:ct * HID],
                                                G[:, c, 0:ct * HID], ALU.add).then_inc(r.hid_added, 1)
                    if n == 0 and not r.fast:
                        with dve.Fori(0, z.tiles) as i:
                            link = Links(dve, sem("slots_dve"), i, 7)
                            col = DSTF[:, bass.ds(i, 1)]
                            hold(dve)
                            v.tensor_copy(ROWS[:, :], col.to_broadcast([P, P])).then_inc(sem("tile_staged"), 1)
                            dve.wait_ge(sem("tile_row"), i + 1)
                            link(v.tensor_tensor(OH[:, 0, 0, :], ROW, col.to_broadcast([P, P]), ALU.is_equal))
                            link(v.tensor_tensor(OH[:, 0, 0, :], OH[:, 0, 0, :], LOWER[:, :], ALU.mult))
                            link(v.tensor_reduce(SMALL[:, 0:1], OH[:, 0, 0, :], AX.X, ALU.add))
                            link(v.tensor_scalar(SMALL[:, 0:1], SMALL[:, 0:1], 0.0, None, ALU.is_gt))
                            link(v.tensor_tensor(SMALL[:, 1:2], TRASH[:, :], col, ALU.subtract))
                            link(v.scalar_tensor_tensor(out=SLOTF[:, bass.ds(i, 1)], in0=SMALL[:, 1:2],
                                                        scalar=SMALL[:, 0:1], in1=col, op0=ALU.mult, op1=ALU.add))
                            hold(dve)
                            link(v.tensor_copy(SLOTI[:, bass.ds(i, 1)], SLOTF[:, bass.ds(i, 1)]))
                            link.end()
                    over_groups(dve, r, body)
                per_route(dve, flag, run)

            def n0(k, first):
                link = Links(dve, sem("n0_link"), k, 8)
                norm("n0", k, link)
                stage("n0", k, 0, part(H, k))
                cells("n0", k)
                finish("n0")
                link.end()
            over_steps(n0)
            dve.wait_ge(phase_done, 1)
            run_pass(0)
            dve.wait_ge(pass_done, 1)

            dve.wait_ge(sem("s17_in"), 16)
            count[0] = 0
            deg = sem("degree_dve")

            def dlink(instruction):
                count[0] += 1
                instruction.then_inc(deg, 1)
                dve.wait_ge(deg, count[0])
            dlink(v.tensor_scalar(INVD[:, :], S17[:, :, 16], 1.0, None, ALU.max))
            dlink(v.reciprocal(INVD[:, :], INVD[:, :]))
            v.tensor_copy(SMALL[:, 3:4], PIDX[:, :]).then_inc(sem("invdeg_ready"), 1)
            dve.wait_ge(sem("invroot_ready"), 1)
            dlink(v.scalar_tensor_tensor(out=DINV[:, :], in0=S17[:, :, 16], scalar=0.0, in1=DINV[:, :],
                                         op0=ALU.is_gt, op1=ALU.mult))

            def spline_out(ph, k, link, h_stage):
                stage(ph, k, 0, part(H, k))
                dve.wait_ge(sem("sums_in"), since(ph, "sums_in") + 16 * (k + 1))
                link(v.tensor_tensor(XC[:, :, :], AG[:, :, 0:F], bc(part(INVD, k), NF), ALU.mult))
                dve.wait_ge(sem(f"{ph}_rf_ps"), k + 1)
                rf = PS[:, R0 * 512:R0 * 512 + NB_STEP * 2 * F].rearrange("p (b w) -> p b w", w=2 * F)
                link(v.tensor_tensor(XC[:, :, :], XC[:, :, :], rf[:, :, 0:F], ALU.add))
                link(v.tensor_scalar(part(H, k), XC[:, :, :], 0.0, None, ALU.max))
                link(v.tensor_tensor(part(X, k), part(X, k), rf[:, :, F:2 * F], ALU.add))

            def n1(k, first):
                link = Links(dve, sem("n1_link"), k, 4)
                spline_out("n1", k, link, True)
                v.tensor_copy(SMALL[:, 3:4], PIDX[:, :]).then_inc(sem("sums_used"), 1)
                stage("n1", k, 1, part(H, k))
                cells("n1", k)
                finish("n1")
                link.end()
            over_steps(n1)
            dve.wait_ge(phase_done, 2)
            run_pass(1)
            dve.wait_ge(pass_done, 2)

            def n2(k, first):
                link = Links(dve, sem("n2_link"), k, 13)
                spline_out("n2", k, link, False)
                v.tensor_copy(SMALL[:, 3:4], PIDX[:, :]).then_inc(sem("sums_used"), 1)
                stage("n2", k, 1, part(H, k))
                dve.wait_ge(sem("n2_f_ps"), k + 1)
                f = PS[:, 6 * 512:6 * 512 + NB_STEP * F].rearrange("p (b w) -> p b w", w=F)
                link(v.tensor_tensor(part(X, k), part(X, k), f, ALU.add))
                if not first:
                    dve.wait_ge(sem("n2_rows_stored"), 16 * k)
                norm("n2", k, link)
                v.tensor_tensor(SQ[:, :, :], part(H, k), bc(part(DINV, k), NF), ALU.mult).then_inc(sem("n2_rows_ready"), 1)
                finish("n2")
                link.end()
            over_steps(n2)
            dve.wait_ge(phase_done, 3)
            run_pass(2)
            dve.wait_ge(pass_done, 3)

            def n3(k, first):
                link = Links(dve, sem("n3_link"), k, 10)
                dve.wait_ge(sem("sums_in"), since("n3", "sums_in") + 16 * (k + 1))
                link(v.tensor_tensor(XC[:, :, :], AG[:, :, 0:F], bc(part(DINV, k), NF), ALU.mult))
                link(v.tensor_tensor(part(X, k), part(X, k), XC[:, :, :], ALU.add))
                v.tensor_copy(SMALL[:, 3:4], PIDX[:, :]).then_inc(sem("sums_used"), 1)
                norm("n3", k, link)
                if not first:
                    dve.wait_ge(sem("n3_q_stored"), 16 * k)
                stage("n3", k, 0, part(H, k))
                finish("n3")
                link.end()
            over_steps(n3)
            dve.wait_ge(phase_done, 4)
            run_pass(3)
            dve.wait_ge(pass_done, 4)

            def n4(k, first):
                link = Links(dve, sem("n4_link"), k, 13)
                link(v.tensor_copy(ST[:, :, 0:F], part(H, k)))
                hold(dve)
                link(v.tensor_copy(TINY[:, 4, :], part(S17, k)[:, :, 16]))
                link(v.tensor_tensor(XC[:, :, :], MB2[:, :].unsqueeze(1).to_broadcast(NF), bc(TINY[:, 4, :], NF),
                                     ALU.mult))
                dve.wait_ge(sem("n4_agg_ps"), k + 1)
                v.tensor_copy(SMALL[:, 3:4], PIDX[:, :]).then_inc(sem("sums_used"), 1)
                agg = PS[:, R0 * 512:R0 * 512 + NB_STEP * F].rearrange("p (b w) -> p b w", w=F)
                v.tensor_tensor(ST[:, :, F:2 * F], agg, XC[:, :, :], ALU.add).then_inc(sem("stage1"), 1)
                dve.wait_ge(sem("n4_y_ps"), k + 1)
                y = PS[:, 6 * 512:6 * 512 + NB_STEP * F].rearrange("p (b w) -> p b w", w=F)
                link(v.tensor_tensor(part(X, k), part(X, k), y, ALU.add))
                link(v.tensor_tensor(part(X, k), part(X, k), UB2[:, :].unsqueeze(1).to_broadcast(NF), ALU.add))
                norm("n4", k, link)
                finish("n4")
                link.end()
            over_steps(n4)

            for l in range(3):
                dve.wait_ge(phase_done, 5 + l)
                run_pass(4 + l)
                dve.wait_ge(pass_done, 5 + l)
                ph = f"n{5 + l}"

                def n5(k, first):
                    link = Links(dve, sem(f"{ph}_link"), k, 3 if l < 2 else 4)
                    link(v.tensor_scalar(TINY[:, 4, :], part(S17, k)[:, :, 16], 1.0, None, ALU.add))
                    link(v.tensor_tensor(ST[:, :, 0:F], part(H, k), bc(TINY[:, 4, :], NF), ALU.mult))
                    dve.wait_ge(sem("sums_in"), since(ph, "sums_in") + 16 * (k + 1))
                    v.tensor_tensor(ST[:, :, F:2 * F], part(H, k), AG[:, :, 0:F], ALU.add).then_inc(sem("stage0"), 1)
                    v.tensor_copy(SMALL[:, 3:4], PIDX[:, :]).then_inc(sem("sums_used"), 1)
                    v.tensor_scalar(XC[:, :, 0:CAT_E], part(S17, k), 1.0, None, ALU.add).then_inc(sem("stage1"), 1)
                    dve.wait_ge(sem(f"{ph}_m_ps"), k + 1)
                    m = PS[:, R0 * 512:R0 * 512 + NB_STEP * F].rearrange("p (b w) -> p b w", w=F)
                    link(v.tensor_scalar(SQ[:, :, :], m, 0.0, None, ALU.max))
                    if l < 2:
                        v.tensor_tensor(part(H, k), SQ[:, :, :], bc(part(MASK, k), NF), ALU.mult
                                        ).then_inc(sem("dve"), 1)
                    else:
                        link(v.tensor_tensor(part(X, k), part(X, k), SQ[:, :, :], ALU.add))
                        finish(ph)
                    link.end()
                over_steps(n5)
                if l == 2:
                    break
                dve.wait_ge(sem("dve"), since(ph, "dve") + z.steps)
                blink = Links(dve, sem(f"{ph}_bn"), 0, 13)
                all_nf = [P, z.blocks, F]
                by_f = "p b f -> p f b"
                v.tensor_reduce(STAT[:, 0, :], H[:, :, :].rearrange(by_f), AX.X, ALU.add
                                ).then_inc(sem(f"{ph}_colsum"), 1)
                dve.wait_ge(sem(f"{ph}_total"), 1)
                blink(v.tensor_scalar(STAT[:, 1, :], bank(7, F), 1.0 / z.nodes, None, ALU.mult))
                blink(v.tensor_tensor(H[:, :, :], H[:, :, :], STAT[:, 1, :].unsqueeze(1).to_broadcast(all_nf),
                                      ALU.subtract))
                blink(v.tensor_tensor(D, H[:, :, :], bc(MASK[:, :], all_nf), ALU.mult))
                blink(v.tensor_tensor(D, D, D, ALU.mult))
                v.tensor_reduce(STAT[:, 0, :], D.rearrange(by_f), AX.X, ALU.add).then_inc(sem(f"{ph}_colsum"), 1)
                dve.wait_ge(sem(f"{ph}_total"), 2)
                blink(v.tensor_scalar(STAT[:, 2, :], bank(7, F), 1.0 / z.nodes, EPS, ALU.mult, ALU.add))
                v.reciprocal(STAT[:, 2, :], STAT[:, 2, :]).then_inc(sem(f"bn{l}_var"), 1)
                dve.wait_ge(sem(f"bn{l}_rstd"), 1)
                blink(v.tensor_tensor(STAT[:, 3, :], STAT[:, 3, :], GAM[:, l, :], ALU.mult))
                blink(v.tensor_tensor(H[:, :, :], H[:, :, :], STAT[:, 3, :].unsqueeze(1).to_broadcast(all_nf),
                                      ALU.mult))
                blink(v.tensor_tensor(H[:, :, :], H[:, :, :], BET[:, l, :].unsqueeze(1).to_broadcast(all_nf),
                                      ALU.add))
                v.tensor_scalar(H[:, :, :], H[:, :, :], 0.0, None, ALU.max).then_inc(sem(f"{ph}_normed"), 1)
                blink.n = 13


sem_loaded_total = [0]


def kernel(**inputs):
    import numpy as np
    import concourse.bacc as bacc
    from concourse.bass_utils import run_bass_kernel_spmd

    a = {n: np.asarray(v) for n, v in inputs.items()}
    nodes, edges = a["x"].shape[0], a["src"].shape[0]
    z = Sizes(nodes, edges)
    padded = z.tiles * P

    def by_tile(v, fill):
        v = v.reshape(edges, -1)
        full = np.full((padded, v.shape[1]), fill, v.dtype)
        full[:edges] = v
        return np.ascontiguousarray(full.reshape(z.groups, P, TILES, -1).transpose(1, 0, 2, 3)
                                    .reshape(P, z.tiles, -1))

    x = np.zeros((z.rows, F), np.float32)
    x[:nodes] = a["x"]
    ea17 = np.ones((P, z.tiles, CAT_E), np.float32)
    ea17[:, :, :16] = by_tile(a["edge_attr_16"], 0)
    w = {
        "x": x, "dst": by_tile(a["dst"], nodes)[:, :, 0], "src": by_tile(a["src"], 0)[:, :, 0],
        "ea2": by_tile(a["edge_attr_2"], 0).reshape(P, -1), "ea17": ea17,
        "ef": by_tile(a["edge_attr_32"], 0).transpose(2, 1, 0).reshape(FEAT_E, -1),
        "roots": a["L0_gnn_roots"], "biases": a["L0_gnn_biases"], "fw": a["L0_gnn_final_w"].T,
        "fb": a["L0_gnn_final_b"][None], "mw1": a["L2_gnn_mW1"], "mb1": a["L2_gnn_mb1"][None],
        "mw2": a["L2_gnn_mW2"], "mb2": a["L2_gnn_mb2"][None], "uw1": a["L2_gnn_uW1"],
        "ub1": a["L2_gnn_ub1"][:, None], "uw2": a["L2_gnn_uW2"], "ub2": a["L2_gnn_ub2"][None],
    }
    for l in range(2):
        w[f"wk{l}"] = a["L0_gnn_weights"][l].transpose(1, 0, 2).reshape(F, 25 * F)
        w[f"g{l}"], w[f"be{l}"] = a[f"L3_gnn_g{l}"][None], a[f"L3_gnn_be{l}"][None]
    for l in range(3):
        w[f"w{l}"], w[f"b{l}"] = a[f"L3_gnn_W{l}"].T, a[f"L3_gnn_b{l}"][None]

    nc = bacc.Bacc("TRN2", target_bir_lowering=False, num_devices=1)
    arrays = {f"in_{n}": np.ascontiguousarray(v) for n, v in w.items()}
    t = {n: nc.dram_tensor(f"in_{n}", arrays[f"in_{n}"].shape, mybir.dt.from_np(arrays[f"in_{n}"].dtype),
                           kind="ExternalInput").ap() for n in w}
    t["out"] = nc.dram_tensor("out", (z.rows, F), F32, kind="ExternalOutput").ap()
    gnn_program(nc, z, t)
    r = run_bass_kernel_spmd(nc, [arrays], core_ids=[0])
    return r.results[0]["out"][:nodes]
```

```python
import concourse.bass as bass
from concourse import mybir
from contextlib import ExitStack

P = 128
F = 64
TILES = 15
CHUNKS = 3
NB_STEP = 9
CELLS = 16
CELL_W = 4 * F
CAT_E = 17
FEAT_E = 32
HID = 128
MIDWAY = 4
EPS = 1e-5

F32 = mybir.dt.float32
I32 = mybir.dt.int32
ALU = mybir.AluOpType
ACT = mybir.ActivationFunctionType
AX = mybir.AxisListType


class Sizes:

    def __init__(self, nodes, edges):
        self.nodes = nodes
        self.groups = -(-edges // (TILES * P))
        self.tiles = self.groups * TILES
        step = P * NB_STEP
        self.rows = -(-(nodes + 1 + P) // step) * step
        self.blocks = self.rows // P
        self.steps = self.blocks // NB_STEP


class Route:

    def __init__(self, name, groups, chunks, chunk_tiles, sem):
        self.name, self.fast = name, name == "fast"
        self.groups, self.chunks, self.chunk_tiles = groups, chunks, chunk_tiles
        self.oh_ready = sem("oh_ready")
        self.chunk_done = sem("chunk_done")
        self.win_staged = sem("win_staged")
        self.slots_staged = sem("slots_staged")
        self.sums_landed = sem("sums_landed")
        self.carry_ready = sem("carry_ready")
        self.prod_ready = sem("prod_ready")
        self.ea_staged = sem("ea_staged")
        self.ea_landed = sem("ea_landed")
        self.oh_turned = sem("oh_turned")
        self.oht_ready = sem("oht_ready")
        self.hid_done = sem("hid_done")
        self.hid_added = sem("hid_added")
        self.hid_ready = sem("hid_ready")
        self.qidx_in = sem("qidx_in")
        self.q_in = sem("q_in")
        self.q_copied = sem("q_copied")
        self.row_staged = sem("row_staged")
        self.row_ready = sem("row_ready")
        self.idx_in = [sem(f"idx_in{c}") for c in range(chunks)]
        self.gathered = [sem(f"gathered{c}") for c in range(chunks)]
        self.ea_in = [sem(f"ea_in{c}") for c in range(chunks)]
        self.ef_in = [sem(f"ef_in{c}") for c in range(chunks)]


class Links:

    def __init__(self, dve, done, step, per_step):
        self.dve, self.done, self.base, self.per_step, self.n = dve, done, step * per_step, per_step, 0

    def __call__(self, instruction):
        self.n += 1
        instruction.then_inc(self.done, 1)
        self.dve.wait_ge(self.done, self.base + self.n)

    def end(self):
        assert self.n == self.per_step, (self.n, self.per_step)


def gnn_program(nc, z, t):
    with ExitStack() as ctx:
        def sb(name, shape, dt=F32):
            return ctx.enter_context(nc.sbuf_tensor(name, shape, dt))

        def dram(name, shape, dt=F32):
            return nc.dram_tensor(name, shape, dt).ap()

        ctx.enter_context(nc.allow_non_contiguous_dma(reason="columns of 128 indices"))
        named = {}
        loads = [0]

        def sem(name):
            if name not in named:
                named[name] = ctx.enter_context(nc.semaphore(name))
            return named[name]

        t_cell = dram("t_cell", (z.rows * CELLS, CELL_W))
        t_gcn = dram("t_gcn", (z.rows, F))
        t_p = dram("t_p", (z.rows, HID))
        t_q = dram("t_q", (z.rows, HID))
        t_mp = [dram(f"t_mp{l}", (z.rows, F)) for l in range(3)]
        cell_idx = dram("cell_idx", (P, z.tiles), I32)
        acc_ea = dram("acc_ea", (z.rows, CAT_E))
        passes = [("spline", t_cell, CELL_W, dram("acc0", (z.rows, CELL_W))),
                  ("spline", t_cell, CELL_W, dram("acc1", (z.rows, CELL_W))),
                  ("sum", t_gcn, F, dram("acc2", (z.rows, F))),
                  ("mlp", t_p, HID, dram("acc3", (z.rows, HID))),
                  ("sum", t_mp[0], F, dram("acc4", (z.rows, F))),
                  ("sum", t_mp[1], F, dram("acc5", (z.rows, F))),
                  ("sum", t_mp[2], F, dram("acc6", (z.rows, F)))]

        X = sb("X", [P, z.blocks, F])
        H = sb("H", [P, z.blocks, F])
        COEF = sb("COEF", [P, max(z.tiles * 4, z.blocks * F)])
        coef = COEF[:, 0:z.tiles * 4].rearrange("p (t s) -> p t s", s=4)
        D = COEF[:, 0:z.blocks * F].rearrange("p (b f) -> p b f", f=F)
        DSTF = sb("DSTF", [P, z.tiles])
        REL = sb("REL", [P, z.tiles])
        SLOTF = sb("SLOTF", [P, z.tiles])
        SLOTI = sb("SLOTI", [P, z.tiles], I32)
        S17 = sb("S17", [P, z.blocks, CAT_E])
        INVD = sb("INVD", [P, z.blocks])
        DINV = sb("DINV", [P, z.blocks])
        MASK = sb("MASK", [P, z.blocks])
        FLAG = sb("FLAG", [P, 1], I32)
        IOTA = sb("IOTA", [P, P])
        PIDX = sb("PIDX", [P, 1])
        TRASH = sb("TRASH", [P, 1])
        IDENT = sb("IDENT", [P, P])
        LOWER = sb("LOWER", [P, P])
        CARRY = sb("CARRY", [P, P])
        DELTA = sb("DELTA", [P, z.groups])
        ROW0 = sb("ROW0", [P, P])
        ONES = sb("ONES", [P, P])
        INT = sb("INT", [P, max(P, z.blocks)], I32)
        TINY = sb("TINY", [P, 8, NB_STEP])
        SMALL = sb("SMALL", [P, 4])
        STAT = sb("STAT", [P, 4, F])
        WK = sb("WK", [F, 25 * F])
        RFW = [sb(f"RFW{l}", [F + 1, 2 * F]) for l in range(2)]
        FW2 = sb("FW2", [F, F])
        MW1 = sb("MW1", [F + 1, 2 * HID])
        MWE = sb("MWE", [FEAT_E, HID])
        MW2 = sb("MW2", [HID, F])
        MB2 = sb("MB2", [P, F])
        UW1 = sb("UW1", [2 * F, HID])
        UB1 = sb("UB1", [HID, 1])
        UW2 = sb("UW2", [HID, F])
        UB2 = sb("UB2", [P, F])
        WDS = sb("WDS", [2 * F, 3, F])
        WE = sb("WE", [CAT_E, 3, F])
        GAM = sb("GAM", [P, 2, F])
        BET = sb("BET", [P, 2, F])
        RING = sb("RING", [P, 2 * CELLS * CELL_W])
        g_end = TILES * CELL_W
        oh_end = g_end + TILES * P
        hs_end = oh_end + TILES * HID
        G = RING[:, 0:g_end].rearrange("p (c w) -> p c w", c=CHUNKS)
        OH = RING[:, g_end:oh_end].rearrange("p (c j e) -> p c j e", c=CHUNKS, e=P)
        HS = RING[:, oh_end:hs_end].rearrange("p (c j e) -> p c j e", c=CHUNKS, e=HID)
        HSC = RING[:, oh_end:hs_end].rearrange("p (c w) -> p c w", c=CHUNKS)
        XW = RING[:, :].rearrange("p (n c) -> p n c", n=2)
        IDX = sb("IDX", [P, CHUNKS, TILES // CHUNKS], I32)
        SIDX = sb("SIDX", [P, 1], I32)
        QIDX = sb("QIDX", [P, 1], I32)
        STG = sb("STG", [P, CELL_W])
        STE = sb("STE", [P, CAT_E])
        EA = sb("EA", [P, CHUNKS, TILES // CHUNKS, CAT_E])
        EF = sb("EF", [FEAT_E, CHUNKS, TILES // CHUNKS * P])
        OHT = sb("OHT", [P, TILES // CHUNKS, P])
        QG = sb("QG", [P, HID])
        QW = sb("QW", [P, HID])
        ROWS = sb("ROWS", [P, P])
        ST = sb("ST", [P, NB_STEP, P])
        HT = sb("HT", [P, NB_STEP * P])
        AG = sb("AG", [P, NB_STEP * CELL_W])
        XC = sb("XC", [P, NB_STEP, F])
        SQ = sb("SQ", [P, NB_STEP, F])
        def sums(width):
            return AG[:, 0:NB_STEP * width].rearrange("p (b c) -> p b c", c=width)

        TP, TQ = [RING[:, n * NB_STEP * HID:(n + 1) * NB_STEP * HID].rearrange("p (b h) -> p b h", h=HID)
                  for n in range(2)]
        UT = sb("UT", [HID, NB_STEP * P])
        T17 = UT

        PS = ctx.enter_context(nc.psum_tensor("PS", [P, 8 * 512], F32))

        def bank(b, cols, rows=P):
            return PS[0:rows, b * 512:b * 512 + cols]

        WIN, WINE, ROW = bank(0, CELL_W), bank(1, CAT_E), bank(6, P)
        OT = bank(2, TILES // CHUNKS * P)
        HIDP = bank(4, TILES // CHUNKS * P)
        psT = bank(0, NB_STEP * P)
        R0 = 3

        per_step = {"turned": (1, 2, 2, 1, 2, 2, 2, 2), "copied": (1, 2, 2, 1, 2, 2, 2, 2),
                    "stage0": (1, 1, 1, 1, 0, 1, 1, 1), "stage1": (0, 1, 1, 0, 1, 1, 1, 1),
                    "sums_in": (0,) + (16,) * 7, "sums_used": (0,) + (1,) * 7, "dve": (1,) * 8,
                    "var": (1, 0, 1, 1, 1), "rstd": (1, 0, 1, 1, 1)}

        def since(ph, what):
            return z.steps * sum(per_step[what][:int(ph[1:])])

        fast = Route("fast", z.groups, CHUNKS, TILES // CHUNKS, sem)
        slow = Route("slow", z.tiles, 1, 1, sem)
        pass_done = sem("pass_done")
        phase_done = sem("phase_done")
        flag_ready = sem("flag_ready")
        turn = sem("turn")

        block = ctx.enter_context(nc.Block())

        def per_route(eng, flag, run):
            with eng.If(flag):
                run(fast)
            with eng.Else():
                run(slow)

        def over_groups(eng, route, body):
            body(0, True)
            with eng.Fori(1, route.groups) as i:
                body(i, False)

        def corner_pairs(v):
            row = bank(R0 + v, 5 * F)
            return bass.AP(row.tensor, row.offset, [row.ap[0], [F, 4], [1, 2 * F]])

        def halves(b, v):
            cells = XW[:, b % 2, :].rearrange("p (v u c) -> p v u c", v=4, u=4)
            upper = [cells[:, v - 1, :, 2 * F:4 * F]] if v > 0 else []
            lower = [cells[:, v, :, 0:2 * F]] if v < 4 else []
            return upper + lower

        def free_cells(eng, ph, k, b):
            mine = (NB_STEP + 1) // 2 if b % 2 == 0 else NB_STEP // 2
            before = k * mine + b // 2
            if isinstance(before, int) and before == 0:
                return
            eng.wait_ge(sem(f"{ph}_cells_stored{b % 2}"), before * 16)

        def hold(eng):
            eng.sem_inc(turn, 1)

        def load_flag(eng):
            eng.wait_ge(flag_ready, 1)
            return eng.value_load(FLAG[0:1, 0:1], min_val=0, max_val=1)

        @block.sync
        def _(sp):
            loaded, zero_ready, zeroed = sem("loaded"), sem("zero_ready"), sem("zeroed")
            todo = [(REL[:, :].bitcast(I32), t["dst"]), (SLOTI[:, :], t["src"]),
                    (X[:, :, :].rearrange("p b f -> p (b f)")[:, 0:z.tiles * 2], t["ea2"]),
                    (WK[:, :], t["wk0"]), (FW2[:, :], t["fw"][2 * F:3 * F, :]),
                    (MW1[0:F, 0:HID], t["mw1"][0:F, :]), (MW1[0:F, HID:2 * HID], t["mw1"][F:2 * F, :]),
                    (MW1[F:F + 1, HID:2 * HID], t["mb1"]), (MWE[:, :], t["mw1"][2 * F:2 * F + FEAT_E, :]),
                    (MW2[:, :], t["mw2"]), (MB2[:, :], t["mb2"].to_broadcast([P, F])),
                    (UW1[:, :], t["uw1"]), (UB1[:, :], t["ub1"]), (UW2[:, :], t["uw2"]),
                    (UB2[:, :], t["ub2"].to_broadcast([P, F])),
                    (RFW[0][F:F + 1, F:2 * F], t["fb"])]
            for l in range(2):
                todo += [(RFW[l][0:F, 0:F], t["roots"][l]), (RFW[l][F:F + 1, 0:F], t["biases"][l:l + 1, :]),
                         (RFW[l][0:F, F:2 * F], t["fw"][l * F:(l + 1) * F, :]),
                         (GAM[:, l, :], t[f"g{l}"].to_broadcast([P, F])),
                         (BET[:, l, :], t[f"be{l}"].to_broadcast([P, F]))]
            for l in range(3):
                todo += [(WDS[:, l, :], t[f"w{l}"][0:2 * F, :]), (WE[0:16, l, :], t[f"w{l}"][2 * F:2 * F + 16, :]),
                         (WE[16:17, l, :], t[f"b{l}"])]
            sp.wait_ge(sem("weights_zeroed"), 2)
            hold(sp)
            for dst, src in todo:
                sp.dma_start(dst, src).then_inc(loaded, 16)
            loads[0] = 16 * len(todo)
            sp.wait_ge(zero_ready, 1)
            hold(sp)

            def zero(acc):
                width = acc.shape[1]
                rows = acc.rearrange("(k p b) c -> p k (b c)", p=P, b=NB_STEP)
                none = AG[:, 0:NB_STEP * width].unsqueeze(1).to_broadcast([P, z.steps, NB_STEP * width])
                sp.dma_start(rows, none).then_inc(zeroed, 16)
            zero(passes[0][3])
            zero(acc_ea)
            sp.wait_ge(sem("cell_ready"), 1)
            hold(sp)
            sp.dma_start(cell_idx, SLOTF[:, :].bitcast(I32)).then_inc(sem("cell_stored"), 16)
            sp.wait_ge(sem("edges_ready"), 1)
            hold(sp)
            sp.dma_start(X[:, :, :], t["x"].rearrange("(b p) f -> p b f", p=P)).then_inc(sem("x_in"), 16)
            sp.wait_ge(zeroed, 32)
            hold(sp)
            sp.wait_ge(sem("cell_stored"), 16)
            hold(sp)
            flag = load_flag(sp)

            def store_cells(ph, k, first):
                for b in range(NB_STEP):
                    sp.wait_ge(sem(f"{ph}_xw_act"), 4 * (k * NB_STEP + b + 1))
                    hold(sp)
                    sp.wait_ge(sem(f"{ph}_xw_dve"), 4 * (k * NB_STEP + b + 1))
                    hold(sp)
                    rows = t_cell.rearrange("(n p u) c -> n p (u c)", p=P, u=CELLS)
                    sp.dma_start(rows[bass.ds(k * NB_STEP + b, 1)].rearrange("n p c -> (n p) c"), XW[:, b % 2, :]
                                 ).then_inc(sem(f"{ph}_cells_stored{b % 2}"), 16)

            def end_phase(ph, stores, dve_steps):
                for s, v in stores:
                    sp.wait_ge(s, v)
                    hold(sp)
                sp.wait_ge(sem("dve"), since(ph, "dve") + dve_steps)
                hold(sp)
                sp.sem_inc(phase_done, 1)

            even, odd = (NB_STEP + 1) // 2 * 16, NB_STEP // 2 * 16

            def load_sums(ph, acc, k, first):
                if not first:
                    sp.wait_ge(sem("sums_used"), since(ph, "sums_used") + k)
                    hold(sp)
                width = acc.shape[1]
                rows = acc.rearrange("(b p) c -> p b c", p=P)
                sp.dma_start(sums(width),
                             rows[:, bass.ds(k * NB_STEP, NB_STEP), :]).then_inc(sem("sums_in"), 16)

            def over_steps(body):
                body(0, True)
                with sp.Fori(1, z.steps) as k:
                    body(k, False)

            def ahead(load, store):
                load(0, True)
                with sp.Fori(0, z.steps - 1) as k:
                    load(k + 1, False)
                    store(k)
                store(z.steps - 1)

            def run_pass(n):
                kind, table, width, acc = passes[n]

                def run(r):
                    base = r.groups * n

                    def body(i, first):
                        for c in range(r.chunks):
                            at = i * (r.chunks * r.chunk_tiles) + c * r.chunk_tiles
                            if not first:
                                sp.wait_ge(r.gathered[c], 16 * r.chunk_tiles * (base + i))
                                hold(sp)
                            src = cell_idx if kind == "spline" else t["src"]
                            sp.dma_start(IDX[:, c, 0:r.chunk_tiles], src[:, bass.ds(at, r.chunk_tiles)]
                                         ).then_inc(r.idx_in[c], 16)
                            if not first and n == 0:
                                sp.wait_ge(r.chunk_done, r.chunks * (base + i - 1) + c + 1)
                                hold(sp)
                            if not first and kind == "mlp":
                                sp.wait_ge(r.hid_done, r.chunks * (i - 1) + c + 1)
                                hold(sp)
                            if n == 0:
                                sp.dma_start(EA[:, c, 0:r.chunk_tiles, :],
                                             t["ea17"][:, bass.ds(at, r.chunk_tiles), :]).then_inc(r.ea_in[c], 16)
                            if kind == "mlp":
                                sp.dma_start(EF[:, c, 0:r.chunk_tiles * P],
                                             t["ef"][:, bass.ds(at * P, r.chunk_tiles * P)]).then_inc(r.ef_in[c], 16)
                                if c == 0:
                                    if not first:
                                        sp.wait_ge(r.q_in, 16 * i)
                                        hold(sp)
                                    sp.dma_start(QIDX[:, :], SLOTI[:, bass.ds(i, 1)]).then_inc(r.qidx_in, 16)
                    def store_window(j):
                        sp.wait_ge(r.win_staged, base + j + 1)
                        hold(sp)
                        if n == 0:
                            sp.wait_ge(r.ea_staged, j + 1)
                            hold(sp)
                        at = sp.value_load(SLOTI[0:1, bass.ds(j, 1)], min_val=0, max_val=z.nodes)
                        sp.dma_start(acc[bass.ds(at, P), :], STG[:, 0:acc.shape[1]]).then_inc(r.sums_landed, 16)
                        if n == 0:
                            sp.dma_start(acc_ea[bass.ds(at, P), :], STE[:, :]).then_inc(r.ea_landed, 16)

                    def fast_body(i, first):
                        body(i, first)
                        if not first:
                            store_window(i - 1)

                    if r.fast:
                        over_groups(sp, r, fast_body)
                        store_window(r.groups - 1)
                    else:
                        over_groups(sp, r, body)
                per_route(sp, flag, run)

            over_steps(lambda k, first: store_cells("n0", k, first))
            end_phase("n0", [(sem("n0_cells_stored0"), z.steps * even), (sem("n0_cells_stored1"), z.steps * odd)],
                      z.steps)
            sp.wait_ge(phase_done, 1)
            hold(sp)
            for kind, table, width, acc in passes[1:]:
                zero(acc)
            run_pass(0)
            sp.wait_ge(zeroed, 16 * (len(passes) + 1))
            hold(sp)
            sp.wait_ge(pass_done, 1)
            hold(sp)
            sp.dma_start(WK[:, :], t["wk1"]).then_inc(sem("wk1_in"), 16)
            sp.dma_start(S17[:, :, :], acc_ea.rearrange("(b p) c -> p b c", p=P)).then_inc(sem("s17_in"), 16)

            ahead(lambda k, first: load_sums("n1", passes[0][3], k, first), lambda k: store_cells("n1", k, False))
            end_phase("n1", [(sem("n1_cells_stored0"), z.steps * even), (sem("n1_cells_stored1"), z.steps * odd)],
                      z.steps)
            run_pass(1)
            sp.wait_ge(pass_done, 2)
            hold(sp)

            def store_rows(ph, table, k, stage, what):
                sp.wait_ge(sem(f"{ph}_{what}_ready"), k + 1)
                hold(sp)
                sp.dma_start(table.rearrange("(b p) c -> p b c", p=P)[:, bass.ds(k * NB_STEP, NB_STEP), :],
                             stage).then_inc(sem(f"{ph}_{what}_stored"), 16)

            ahead(lambda k, first: load_sums("n2", passes[1][3], k, first),
                  lambda k: store_rows("n2", t_gcn, k, SQ[:, :, :], "rows"))
            end_phase("n2", [(sem("n2_rows_stored"), 16 * z.steps)], z.steps)
            run_pass(2)
            sp.wait_ge(pass_done, 3)
            hold(sp)

            def store_messages(k):
                store_rows("n3", t_p, k, TP[:, :, :], "p")
                store_rows("n3", t_q, k, TQ[:, :, :], "q")
            ahead(lambda k, first: load_sums("n3", passes[2][3], k, first), store_messages)
            end_phase("n3", [(sem("n3_p_stored"), 16 * z.steps), (sem("n3_q_stored"), 16 * z.steps)], z.steps)
            run_pass(3)
            sp.wait_ge(pass_done, 4)
            hold(sp)
            over_steps(lambda k, first: load_sums("n4", passes[3][3], k, first))
            sp.wait_ge(sem("dve"), since("n4", "dve") + z.steps)
            hold(sp)
            sp.dma_start(t_mp[0].rearrange("(b p) c -> p b c", p=P), H[:, :, :]).then_inc(sem("mp0_stored"), 16)
            end_phase("n4", [(sem("mp0_stored"), 16)], z.steps)
            for l in range(3):
                run_pass(4 + l)
                sp.wait_ge(pass_done, 5 + l)
                hold(sp)
                ph = f"n{5 + l}"
                over_steps(lambda k, first: load_sums(ph, passes[4 + l][3], k, first))
                if l < 2:
                    sp.wait_ge(sem(f"{ph}_normed"), 1)
                    hold(sp)
                    sp.dma_start(t_mp[l + 1].rearrange("(b p) c -> p b c", p=P), H[:, :, :]
                                 ).then_inc(sem(f"mp{l + 1}_stored"), 16)
                    end_phase(ph, [(sem(f"mp{l + 1}_stored"), 16)], z.steps)
            sp.wait_ge(sem("dve"), since("n7", "dve") + z.steps)
            hold(sp)
            sp.dma_start(t["out"].rearrange("(b p) f -> p b f", p=P), X[:, :, :]).then_inc(sem("out_stored"), 16)
            sp.wait_ge(sem("out_stored"), 16)
            hold(sp)

        @block.gpsimd
        def _(pool):
            ints = sem("ints")
            nc.gpsimd.iota(INT[:, 0:P], pattern=[[1, P]], base=0, channel_multiplier=0).then_inc(ints, 1)
            pool.wait_ge(ints, 1)
            nc.gpsimd.tensor_copy(IOTA[:, :], INT[:, 0:P]).then_inc(ints, 1)
            pool.wait_ge(ints, 2)
            nc.gpsimd.iota(INT[:, 0:z.blocks], pattern=[[P, z.blocks]], base=0, channel_multiplier=1).then_inc(ints, 1)
            pool.wait_ge(ints, 3)
            nc.gpsimd.tensor_copy(MASK[:, :], INT[:, 0:z.blocks]).then_inc(sem("iota_ready"), 1)
            flag = load_flag(pool)

            def run_pass(n):
                kind, table, width, acc = passes[n]

                def run(r):
                    base = r.groups * n
                    ct = r.chunk_tiles

                    def scatter(j):
                        pool.wait_ge(r.win_staged, base + j + 1)
                        pool.wait_ge(r.slots_staged, base + j + 1)
                        if n == 0:
                            pool.wait_ge(r.ea_staged, j + 1)
                        hold(pool)
                        to = bass.IndirectOffsetOnAxis(ap=SIDX[:, 0:1], axis=0)
                        nc.gpsimd.indirect_dma_start(acc, to, STG[:, 0:acc.shape[1]], None,
                                                     compute_op=ALU.add).then_inc(r.sums_landed, 16)
                        if n == 0:
                            nc.gpsimd.indirect_dma_start(acc_ea, to, STE[:, :], None,
                                                         compute_op=ALU.add).then_inc(r.ea_landed, 16)

                    def body(i, first):
                        if kind == "mlp":
                            pool.wait_ge(r.qidx_in, 16 * (i + 1))
                            if not first:
                                pool.wait_ge(r.q_copied, i)
                            hold(pool)
                            nc.gpsimd.indirect_dma_start(QG[:, :], None, t_q, bass.IndirectOffsetOnAxis(
                                ap=QIDX[:, 0:1], axis=0)).then_inc(r.q_in, 16)
                        for c in range(r.chunks):
                            pool.wait_ge(r.idx_in[c], 16 * (base + i + 1))
                            if not first:
                                pool.wait_ge(r.chunk_done, r.chunks * (base + i - 1) + c + 1)
                            hold(pool)
                            for j in range(ct):
                                nc.gpsimd.indirect_dma_start(
                                    G[:, c, j * width:(j + 1) * width], None, table,
                                    bass.IndirectOffsetOnAxis(ap=IDX[:, c, j:j + 1], axis=0)
                                ).then_inc(r.gathered[c], 16)
                        if not r.fast and not first:
                            scatter(i - 1)
                    over_groups(pool, r, body)
                    if not r.fast:
                        scatter(r.groups - 1)
                    pool.wait_ge(r.sums_landed, 16 * (base + r.groups))
                    if n == 0:
                        pool.wait_ge(r.ea_landed, 16 * r.groups)
                    pool.sem_inc(pass_done, 1)
                per_route(pool, flag, run)

            for n in range(len(passes)):
                pool.wait_ge(phase_done, n + 1)
                run_pass(n)

        @block.tensor
        def _(pe):
            pe.wait_ge(sem("dst_ready"), 1)
            nc.tensor.matmul(bank(7, z.groups), ROW0[:, :],
                             DSTF[:, :].rearrange("p (g j) -> p g j", j=TILES)[:, :, 0],
                             start=True, stop=True).then_inc(sem("base_ps"), 1)
            pe.wait_ge(sem("misfits_ready"), 1)
            nc.tensor.matmul(bank(7, 1), ONES[:, :], SMALL[:, 0:1], start=True, stop=True
                             ).then_inc(sem("misfits_ps"), 1)
            flag = load_flag(pe)

            def turn(ph, k, r, rounds, src, cols, wait=True):
                pe.wait_ge(sem(f"stage{r}"), since(ph, f"stage{r}") + k + 1)
                hold(pe)
                for b in range(NB_STEP):
                    last = nc.tensor.transpose(psT[0:cols, b * P:(b + 1) * P], src[:, b, 0:cols], IDENT[:, :])
                last.then_inc(sem("turned"), 1)
                if wait:
                    pe.wait_ge(sem("copied"), since(ph, "copied") + rounds * k + r + 1)

            def cells(ph, k, first, before_last=None):
                for b in range(NB_STEP):
                    if b == NB_STEP - 1 and before_last:
                        before_last()
                    for v in range(5):
                        if not (first and b == 0):
                            copied = sem(f"{ph}_xw_dve" if v % 2 else f"{ph}_xw_act")
                            pe.wait_ge(copied, 4 * (k * NB_STEP + b - 1) + (1, 2, 3, 4, 4)[v])
                        nc.tensor.matmul(bank(R0 + v, 5 * F), HT[0:F, b * P:(b + 1) * P],
                                         WK[:, v * 5 * F:(v + 1) * 5 * F], start=True, stop=True
                                         ).then_inc(sem(f"{ph}_xw_ps"), 1)

            def products(ph, k, what, lhs, rhs, width, per_bank, at=R0):
                for b in range(NB_STEP):
                    col = (at + b // per_bank) * 512 + b % per_bank * width
                    for n, (lh, rh) in enumerate(zip(lhs, rhs)):
                        last = nc.tensor.matmul(PS[:, col:col + width], lh[:, b * P:(b + 1) * P], rh,
                                                start=(n == 0), stop=(n == len(lhs) - 1))
                last.then_inc(sem(f"{ph}_{what}"), 1)

            def over_steps(body):
                body(0, True)
                with pe.Fori(1, z.steps) as k:
                    body(k, False)

            def run_pass(n):
                kind, table, width, acc = passes[n]
                out_w = acc.shape[1]

                def run(r):
                    base = r.groups * n
                    ct = r.chunk_tiles

                    def row(i):
                        if not r.fast:
                            pe.wait_ge(r.row_staged, base + i + 1)
                            nc.tensor.matmul(ROW, ROWS[:, :], IDENT[:, :], start=True, stop=True
                                             ).then_inc(r.row_ready, 1)

                    def carry(i):
                        pe.wait_ge(r.carry_ready, (r.groups - 1) * n + i)
                        if n == 0:
                            nc.tensor.matmul(WINE, CARRY[:, :], STE[:, :], start=True, stop=False)
                        nc.tensor.matmul(WIN[:, 0:out_w], CARRY[:, :], STG[:, 0:out_w], start=True, stop=False)

                    def sum_chunk(c, src, w, carried):
                        for j in range(ct):
                            last = nc.tensor.matmul(WIN[:, 0:out_w], OH[:, c, j, :], src[:, c, j * w:(j + 1) * w],
                                                    start=(c == 0 and j == 0 and not carried),
                                                    stop=(c == r.chunks - 1 and j == ct - 1))
                        last.then_inc(r.chunk_done, 1)

                    def body(i, first):
                        for c in range(r.chunks):
                            row(i)
                            pe.wait_ge(r.oh_ready, r.chunks * (base + i) + c + 1)
                            if kind == "spline":
                                pe.wait_ge(r.prod_ready, r.chunks * (base + i) + c + 1)
                            else:
                                pe.wait_ge(r.gathered[c], 16 * ct * (base + i + 1))
                            if n == 0:
                                pe.wait_ge(r.ea_in[c], 16 * (i + 1))
                            if c == 0 and not first:
                                pe.wait_ge(r.win_staged, base + i)
                                if n == 0:
                                    pe.wait_ge(r.ea_staged, i)
                            carried = r.fast and not first
                            if carried and c == 0:
                                carry(i)
                            if n == 0:
                                for j in range(ct):
                                    nc.tensor.matmul(WINE, OH[:, c, j, :], EA[:, c, j, :],
                                                     start=(c == 0 and j == 0 and not carried),
                                                     stop=(c == r.chunks - 1 and j == ct - 1))
                            sum_chunk(c, G, width, carried)

                    def sum_hidden(i, c, first):
                        pe.wait_ge(r.hid_ready, r.chunks * i + c + 1)
                        if c == 0:
                            pe.wait_ge(r.win_staged, base + i)
                        carried = r.fast and not first
                        if carried and c == 0:
                            carry(i)
                        sum_chunk(c, HSC, HID, carried)

                    def mlp_body(i, first):
                        for c in range(r.chunks):
                            row(i)
                            pe.wait_ge(r.oh_ready, r.chunks * (base + i) + c + 1)
                            for j in range(ct):
                                last = nc.tensor.transpose(OT[:, j * P:(j + 1) * P], OH[:, c, j, :], IDENT[:, :])
                            last.then_inc(r.oh_turned, 1)
                            pe.wait_ge(r.ef_in[c], 16 * (i + 1))
                            if c == 0:
                                pe.wait_ge(r.q_copied, i + 1)
                            if not (first and c == 0):
                                pe.wait_ge(r.hid_added, r.chunks * i + c)
                            pe.wait_ge(r.oht_ready, r.chunks * i + c + 1)
                            for j in range(ct):
                                nc.tensor.matmul(HIDP[:, j * HID:(j + 1) * HID], EF[:, c, j * P:(j + 1) * P],
                                                 MWE[:, :], start=True, stop=False)
                                last = nc.tensor.matmul(HIDP[:, j * HID:(j + 1) * HID], OHT[:, j, :],
                                                        QW[:, :], start=False, stop=True)
                            last.then_inc(r.hid_done, 1)
                            if not r.fast:
                                sum_hidden(i, c, first)
                            elif c > 0:
                                sum_hidden(i, c - 1, first)
                            elif not first:
                                sum_hidden(i - 1, r.chunks - 1, False)
                    if n == 0 and not r.fast:
                        with pe.Fori(0, z.tiles) as i:
                            pe.wait_ge(sem("tile_staged"), i + 1)
                            nc.tensor.matmul(ROW, ROWS[:, :], IDENT[:, :], start=True, stop=True
                                             ).then_inc(sem("tile_row"), 1)
                    if kind == "mlp":
                        over_groups(pe, r, mlp_body)
                        if r.fast:
                            sum_hidden(r.groups - 1, r.chunks - 1, False)
                    else:
                        over_groups(pe, r, body)
                per_route(pe, flag, run)

            def n0(k, first, last):
                pe.wait_ge(sem("copied"), k + 1)
                cells("n0", k, first, None if last else lambda: turn("n0", k + 1, 0, 1, ST, F, False))
            turn("n0", 0, 0, 1, ST, F, False)
            n0(0, True, False)
            with pe.Fori(1, z.steps - 1) as k:
                n0(k, False, False)
            n0(z.steps - 1, False, True)
            pe.wait_ge(phase_done, 1)
            run_pass(0)
            pe.wait_ge(pass_done, 1)
            pe.wait_ge(sem("wk1_in"), 16)

            def n1(k, first):
                turn("n1", k, 0, 2, ST, F)
                if not first:
                    pe.wait_ge(sem("n1_xw_act"), k * 4 * NB_STEP)
                    pe.wait_ge(sem("n1_xw_dve"), k * 4 * NB_STEP)
                products("n1", k, "rf_ps", [HT[0:F + 1, :]], [RFW[0][:, :]], 2 * F, 4)
                turn("n1", k, 1, 2, ST, F)
                cells("n1", k, first)
            over_steps(n1)
            pe.wait_ge(phase_done, 2)
            run_pass(1)
            pe.wait_ge(pass_done, 2)

            def n2(k, first):
                turn("n2", k, 0, 2, ST, F)
                products("n2", k, "rf_ps", [HT[0:F + 1, :]], [RFW[1][:, :]], 2 * F, 4)
                turn("n2", k, 1, 2, ST, F)
                products("n2", k, "f_ps", [HT[0:F, :]], [FW2[:, :]], F, 8, 6)
            over_steps(n2)
            pe.wait_ge(phase_done, 3)
            run_pass(2)
            pe.wait_ge(pass_done, 3)

            def n3(k, first):
                turn("n3", k, 0, 1, ST, F)
                if not first:
                    pe.wait_ge(sem("n3_q_ready"), k)
                products("n3", k, "pq_ps", [HT[0:F + 1, :]], [MW1[:, :]], 2 * HID, 2)
            over_steps(n3)
            pe.wait_ge(phase_done, 4)
            run_pass(3)
            pe.wait_ge(pass_done, 4)

            def n4(k, first):
                pe.wait_ge(sem("sums_in"), since("n4", "sums_in") + 16 * (k + 1))
                for b in range(NB_STEP):
                    last = nc.tensor.transpose(psT[:, b * P:(b + 1) * P], sums(HID)[:, b, :], IDENT[:, :])
                last.then_inc(sem("turned"), 1)
                pe.wait_ge(sem("copied"), since("n4", "copied") + 2 * k + 1)
                products("n4", k, "agg_ps", [HT[:, :]], [MW2[:, :]], F, 8)
                turn("n4", k, 1, 2, ST, P)
                for j in range(NB_STEP // 3):
                    last = nc.tensor.matmul(bank(R0 + j, 3 * P), UW1[:, :], HT[:, j * 3 * P:(j + 1) * 3 * P],
                                            start=True, stop=True)
                last.then_inc(sem("n4_u_ps"), 1)
                pe.wait_ge(sem("n4_u_ready"), k + 1)
                if not first:
                    pe.wait_ge(sem("n4_updated"), k)
                products("n4", k, "y_ps", [UT[:, :]], [UW2[:, :]], F, 8, 6)
            over_steps(n4)
            for l in range(3):
                pe.wait_ge(phase_done, 5 + l)
                run_pass(4 + l)
                pe.wait_ge(pass_done, 5 + l)
                ph = f"n{5 + l}"

                def n5(k, first):
                    turn(ph, k, 0, 2, ST, P)
                    turn(ph, k, 1, 2, XC, CAT_E)
                    if not first:
                        pe.wait_ge(sem("dve"), since(ph, "dve") + k)
                    products(ph, k, "m_ps", [HT[:, :], T17[0:CAT_E, :]], [WDS[:, l, :], WE[:, l, :]], F, 8)
                over_steps(n5)
                if l < 2:
                    for s in range(2):
                        pe.wait_ge(sem(f"{ph}_colsum"), s + 1)
                        nc.tensor.matmul(bank(7, F), ONES[:, :], STAT[:, 0, :], start=True, stop=True
                                         ).then_inc(sem(f"{ph}_total"), 1)

        @block.scalar
        def _(act):
            copy = ACT.Copy

            def turned(ph, k, r, rounds, rows, to=HT):
                act.wait_ge(sem("turned"), since(ph, "turned") + rounds * k + r + 1)
                nc.scalar.activation(to[0:rows, :], psT[0:rows, :], copy).then_inc(sem("copied"), 1)

            def root(ph, k):
                act.wait_ge(sem("var"), since(ph, "var") + k + 1)
                nc.scalar.activation(TINY[:, 3, :], TINY[:, 2, :], ACT.Sqrt).then_inc(sem("rstd"), 1)

            def cells(ph, k, midway=None):
                for b in range(NB_STEP):
                    if b == MIDWAY and midway:
                        midway()
                    free_cells(act, ph, k, b)
                    for v in range(0, 5, 2):
                        act.wait_ge(sem(f"{ph}_xw_ps"), k * 5 * NB_STEP + 5 * b + v + 1)
                        for half in halves(b, v):
                            nc.scalar.activation(half, corner_pairs(v), copy).then_inc(sem(f"{ph}_xw_act"), 1)

            def over_steps(body):
                body(0, True)
                with act.Fori(1, z.steps) as k:
                    body(k, False)

            def run_pass(n):
                kind, table, width, acc = passes[n]
                out_w = acc.shape[1]

                def run(r):
                    base = r.groups * n

                    def stage_window(i, first):
                        act.wait_ge(r.chunk_done, r.chunks * (base + i + 1))
                        if not first:
                            act.wait_ge(r.sums_landed, 16 * (base + i))
                            if n == 0:
                                act.wait_ge(r.ea_landed, 16 * i)
                        if n == 0:
                            nc.scalar.activation(STE[:, :], WINE, copy).then_inc(r.ea_staged, 1)
                        nc.scalar.activation(STG[:, 0:out_w], WIN[:, 0:out_w], copy).then_inc(r.win_staged, 1)
                        if not r.fast:
                            nc.scalar.activation(SIDX[:, :], SLOTI[:, bass.ds(i, 1)], copy
                                                 ).then_inc(r.slots_staged, 1)

                    def mlp_body(i, first):
                        act.wait_ge(r.q_in, 16 * (i + 1))
                        if not first:
                            act.wait_ge(r.hid_done, r.chunks * i)
                        nc.scalar.activation(QW[:, :], QG[:, :], copy).then_inc(r.q_copied, 1)
                        for c in range(r.chunks):
                            act.wait_ge(r.oh_turned, r.chunks * i + c + 1)
                            nc.scalar.activation(OHT[:, 0:r.chunk_tiles, :],
                                                 OT.rearrange("p (j e) -> p j e", e=P)[:, 0:r.chunk_tiles, :],
                                                 copy).then_inc(r.oht_ready, 1)
                            act.wait_ge(r.hid_added, r.chunks * i + c + 1)
                            nc.scalar.activation(HS[:, c, 0:r.chunk_tiles, :], HS[:, c, 0:r.chunk_tiles, :],
                                                 ACT.Relu).then_inc(r.hid_ready, 1)
                            if c == 0 and r.fast and not first:
                                stage_window(i - 1, False)
                        if not r.fast:
                            stage_window(i, first)

                    if kind == "mlp":
                        over_groups(act, r, mlp_body)
                        if r.fast:
                            stage_window(r.groups - 1, False)
                    else:
                        over_groups(act, r, stage_window)
                per_route(act, flag, run)

            flag = load_flag(act)

            def n0(k, first, last):
                if not first:
                    act.wait_ge(sem("n0_xw_ps"), k * 5 * NB_STEP)
                turned("n0", k, 0, 1, F)
                cells("n0", k, None if last else lambda: root("n0", k + 1))
            root("n0", 0)
            n0(0, True, False)
            with act.Fori(1, z.steps - 1) as k:
                n0(k, False, False)
            n0(z.steps - 1, False, True)
            act.wait_ge(phase_done, 1)
            run_pass(0)
            act.wait_ge(pass_done, 1)
            act.wait_ge(sem("invdeg_ready"), 1)
            nc.scalar.activation(DINV[:, :], INVD[:, :], ACT.Sqrt).then_inc(sem("invroot_ready"), 1)

            def n1(k, first):
                turned("n1", k, 0, 2, F)
                turned("n1", k, 1, 2, F)
                cells("n1", k)
            over_steps(n1)
            act.wait_ge(phase_done, 2)
            run_pass(1)
            act.wait_ge(pass_done, 2)

            def n2(k, first):
                turned("n2", k, 0, 2, F)
                turned("n2", k, 1, 2, F)
                root("n2", k)
            over_steps(n2)
            act.wait_ge(phase_done, 3)
            run_pass(2)
            act.wait_ge(pass_done, 3)

            def n3(k, first):
                root("n3", k)
                turned("n3", k, 0, 1, F)
                act.wait_ge(sem("n3_pq_ps"), k + 1)
                if not first:
                    act.wait_ge(sem("n3_p_stored"), 16 * k)
                    act.wait_ge(sem("n3_q_stored"), 16 * k)
                for j in range(-(-NB_STEP // 2)):
                    m = min(2, NB_STEP - 2 * j)
                    src = bank(R0 + j, m * 2 * HID).rearrange("p (b w) -> p b w", w=2 * HID)
                    last = nc.scalar.activation(TP[:, 2 * j:2 * j + m, :], src[:, :, 0:HID], copy)
                last.then_inc(sem("n3_p_ready"), 1)
                for j in range(-(-NB_STEP // 2)):
                    m = min(2, NB_STEP - 2 * j)
                    src = bank(R0 + j, m * 2 * HID).rearrange("p (b w) -> p b w", w=2 * HID)
                    last = nc.scalar.activation(TQ[:, 2 * j:2 * j + m, :], src[:, :, HID:2 * HID], copy)
                last.then_inc(sem("n3_q_ready"), 1)
            over_steps(n3)
            act.wait_ge(phase_done, 4)
            run_pass(3)
            act.wait_ge(pass_done, 4)

            def n4(k, first):
                turned("n4", k, 0, 2, P)
                turned("n4", k, 1, 2, P)
                act.wait_ge(sem("n4_u_ps"), k + 1)
                for j in range(NB_STEP // 3):
                    last = nc.scalar.activation(UT[:, j * 3 * P:(j + 1) * 3 * P], bank(R0 + j, 3 * P), ACT.Relu,
                                                bias=UB1[:, 0:1])
                last.then_inc(sem("n4_u_ready"), 1)
                if not first:
                    root("n4", k - 1)
            over_steps(n4)
            root("n4", z.steps - 1)
            for l in range(3):
                act.wait_ge(phase_done, 5 + l)
                run_pass(4 + l)
                act.wait_ge(pass_done, 5 + l)
                ph = f"n{5 + l}"

                def n5(k, first):
                    turned(ph, k, 0, 2, P)
                    turned(ph, k, 1, 2, CAT_E, T17)
                over_steps(n5)
                if l < 2:
                    act.wait_ge(sem(f"bn{l}_var"), 1)
                    nc.scalar.activation(STAT[:, 3, :], STAT[:, 2, :], ACT.Sqrt).then_inc(sem(f"bn{l}_rstd"), 1)

        @block.vector
        def _(dve):
            v = nc.vector
            setup = sem("setup_dve")
            count = [0]

            def link(instruction):
                count[0] += 1
                instruction.then_inc(setup, 1)
                dve.wait_ge(setup, count[0])

            def bc(ap, shape):
                return ap.unsqueeze(2).to_broadcast(shape)

            v.memset(MW1[F:F + 1, 0:HID], 0.0).then_inc(sem("weights_zeroed"), 1)
            v.memset(RFW[1][F:F + 1, F:2 * F], 0.0).then_inc(sem("weights_zeroed"), 1)
            link(v.memset(ONES[:, :], 1.0))
            link(v.memset(HT[F:F + 1, :], 1.0))
            v.memset(AG[:, :], 0.0).then_inc(sem("zero_ready"), 1)
            dve.wait_ge(sem("iota_ready"), 1)
            link(v.tensor_copy(PIDX[:, :], MASK[:, 0:1]))
            link(v.tensor_scalar(TRASH[:, :], PIDX[:, :], float(z.nodes + 1), None, ALU.add))
            link(v.tensor_scalar(MASK[:, :], MASK[:, :], float(z.nodes), None, ALU.is_lt))
            link(v.tensor_scalar(IDENT[:, :], IOTA[:, :], PIDX[:, 0:1], None, ALU.is_equal))
            link(v.tensor_scalar(LOWER[:, :], IOTA[:, :], PIDX[:, 0:1], None, ALU.is_lt))
            link(v.tensor_scalar(ROW0[:, :], ONES[:, :], IDENT[:, 0:1], None, ALU.mult))
            dve.wait_ge(sem("loaded"), loads[0])
            link(v.tensor_copy(DSTF[:, :], REL[:, :].bitcast(I32)))
            v.tensor_copy(SMALL[:, 3:4], DSTF[:, 0:1]).then_inc(sem("dst_ready"), 1)
            dve.wait_ge(sem("base_ps"), 1)
            base = STAT[:, 0:4, :].rearrange("p a f -> p (a f)")[:, 0:z.groups]
            link(v.tensor_copy(base, bank(7, z.groups)))
            in_groups = "p (g j) -> p g j"
            link(v.tensor_tensor(REL[:, :].rearrange(in_groups, j=TILES), DSTF[:, :].rearrange(in_groups, j=TILES),
                                 bc(base, [P, z.groups, TILES]), ALU.subtract))
            flat = COEF[:, 0:z.tiles]
            link(v.tensor_scalar(flat, REL[:, :], 0.0, None, ALU.is_lt))
            link(v.tensor_reduce(SMALL[:, 1:2], flat, AX.X, ALU.add))
            link(v.tensor_scalar(flat, REL[:, :], float(P), None, ALU.is_ge))
            link(v.tensor_reduce(SMALL[:, 2:3], flat, AX.X, ALU.add))
            link(v.tensor_tensor(SMALL[:, 1:2], SMALL[:, 1:2], SMALL[:, 2:3], ALU.add))
            link(v.memset(DELTA[:, 0:1], 0.0))
            link(v.tensor_tensor(DELTA[:, 1:], base[:, 0:z.groups - 1], base[:, 1:], ALU.subtract))
            link(v.tensor_scalar(flat[:, 0:z.groups], DELTA[:, :], 0.0, None, ALU.is_gt))
            link(v.tensor_reduce(SMALL[:, 2:3], flat[:, 0:z.groups], AX.X, ALU.add))
            link(v.tensor_scalar(DELTA[:, :], DELTA[:, :], PIDX[:, 0:1], None, ALU.add))
            v.tensor_tensor(SMALL[:, 0:1], SMALL[:, 1:2], SMALL[:, 2:3], ALU.add).then_inc(sem("misfits_ready"), 1)
            ev = X[:, :, :].rearrange("p b f -> p (b f)")[:, 0:z.tiles * 2]
            fl = H[:, :, :].rearrange("p b f -> p (b f)")[:, 0:z.tiles * 2]
            link(v.tensor_scalar(ev, ev, 4.0, 0.0, ALU.mult, ALU.max))
            link(v.tensor_scalar(ev, ev, 4.0, None, ALU.min))
            link(v.tensor_scalar(fl, ev, 1.0, None, ALU.is_ge))
            for edge in (2.0, 3.0):
                link(v.scalar_tensor_tensor(out=fl, in0=ev, scalar=edge, in1=fl, op0=ALU.is_ge, op1=ALU.add))
            link(v.tensor_tensor(ev, ev, fl, ALU.subtract))
            f2 = fl.rearrange("p (t d) -> p t d", d=2)
            e2 = ev.rearrange("p (t d) -> p t d", d=2)
            link(v.scalar_tensor_tensor(out=flat, in0=f2[:, :, 1], scalar=4.0, in1=f2[:, :, 0],
                                        op0=ALU.mult, op1=ALU.add))
            link(v.tensor_copy(SLOTF[:, :], SLOTI[:, :]))
            link(v.scalar_tensor_tensor(out=flat, in0=SLOTF[:, :], scalar=float(CELLS), in1=flat,
                                        op0=ALU.mult, op1=ALU.add))
            link(v.tensor_copy(SLOTF[:, :].bitcast(I32), flat))
            link(v.tensor_scalar(fl, ev, -1.0, 1.0, ALU.mult, ALU.add))
            v.tensor_copy(SMALL[:, 3:4], PIDX[:, :]).then_inc(sem("cell_ready"), 1)
            for s, (a, b) in enumerate([(f2, f2), (e2, f2), (f2, e2), (e2, e2)]):
                link(v.tensor_tensor(coef[:, :, s], a[:, :, 0], b[:, :, 1], ALU.mult))
            v.tensor_copy(SMALL[:, 3:4], PIDX[:, :]).then_inc(sem("edges_ready"), 1)
            link(v.tensor_scalar(base, base, PIDX[:, 0:1], None, ALU.add))
            link(v.tensor_copy(SLOTI[:, 0:z.groups], base))
            dve.wait_ge(sem("misfits_ps"), 1)
            link(v.tensor_scalar(SMALL[:, 0:1], bank(7, 1), 0.5, None, ALU.is_lt))
            v.tensor_copy(FLAG[:, :], SMALL[:, 0:1]).then_inc(flag_ready, 1)
            dve.wait_ge(sem("x_in"), 16)
            flag = load_flag(dve)

            NF = [P, NB_STEP, F]

            def over_steps(body):
                body(0, True)
                with dve.Fori(1, z.steps) as k:
                    body(k, False)

            def part(a, k):
                return a[:, bass.ds(k * NB_STEP, NB_STEP)]

            def norm(ph, k, link):
                x = part(X, k)
                hold(dve)
                link(v.tensor_reduce(TINY[:, 0, :], x, AX.X, ALU.add))
                link(v.tensor_scalar(TINY[:, 0, :], TINY[:, 0, :], 1.0 / F, None, ALU.mult))
                link(v.tensor_tensor(XC[:, :, :], x, bc(TINY[:, 0, :], NF), ALU.subtract))
                link(v.tensor_tensor(SQ[:, :, :], XC[:, :, :], XC[:, :, :], ALU.mult))
                link(v.tensor_reduce(TINY[:, 1, :], SQ[:, :, :], AX.X, ALU.add))
                link(v.tensor_scalar(TINY[:, 1, :], TINY[:, 1, :], 1.0 / F, EPS, ALU.mult, ALU.add))
                v.reciprocal(TINY[:, 2, :], TINY[:, 1, :]).then_inc(sem("var"), 1)
                dve.wait_ge(sem("rstd"), since(ph, "rstd") + k + 1)
                link(v.tensor_scalar(XC[:, :, :], XC[:, :, :], 0.0, None, ALU.max))
                link(v.tensor_tensor(part(H, k), XC[:, :, :], bc(TINY[:, 3, :], NF), ALU.mult))

            def cells(ph, k, midway=None):
                for b in range(NB_STEP):
                    if b == MIDWAY and midway:
                        midway()
                    free_cells(dve, ph, k, b)
                    for q in range(1, 5, 2):
                        dve.wait_ge(sem(f"{ph}_xw_ps"), k * 5 * NB_STEP + 5 * b + q + 1)
                        for half in halves(b, q):
                            v.tensor_copy(half, corner_pairs(q)).then_inc(sem(f"{ph}_xw_dve"), 1)

            def stage(ph, k, r, src, to=None):
                hold(dve)
                v.tensor_copy(ST[:, :, 0:F] if to is None else to, src).then_inc(sem(f"stage{r}"), 1)

            def finish(ph):
                v.tensor_copy(SMALL[:, 3:4], PIDX[:, :]).then_inc(sem("dve"), 1)

            def run_pass(n):
                kind, table, width, acc = passes[n]

                def run(r):
                    base = r.groups * n
                    ct = r.chunk_tiles

                    def add_rows(i, c):
                        dve.wait_ge(r.gathered[c], 16 * ct * (base + i + 1))
                        dve.wait_ge(r.hid_done, r.chunks * i + c + 1)
                        v.tensor_tensor(HSC[:, c, 0:ct * HID], HIDP[:, 0:ct * HID],
                                        G[:, c, 0:ct * HID], ALU.add).then_inc(r.hid_added, 1)

                    def body(i, first):
                        for c in range(r.chunks):
                            at = i * (r.chunks * ct) + c * ct
                            shape = [P, ct, P]
                            if not first:
                                dve.wait_ge(r.chunk_done, r.chunks * (base + i - 1) + c + 1)
                            if r.fast:
                                of, slots = REL, IOTA[:, :]
                                if c == 0 and not first:
                                    v.tensor_tensor(CARRY[:, :], IOTA[:, :],
                                                    DELTA[:, bass.ds(i, 1)].to_broadcast([P, P]), ALU.is_equal
                                                    ).then_inc(r.carry_ready, 1)
                            else:
                                hold(dve)
                                v.tensor_copy(ROWS[:, :], SLOTF[:, bass.ds(i, 1)].to_broadcast([P, P])
                                              ).then_inc(r.row_staged, 1)
                                dve.wait_ge(r.row_ready, base + i + 1)
                                of, slots = DSTF, ROW
                            v.tensor_tensor(OH[:, c, 0:ct, :], bc(of[:, bass.ds(at, ct)], shape),
                                            slots.unsqueeze(1).to_broadcast(shape), ALU.is_equal).then_inc(r.oh_ready, 1)
                            if kind == "spline":
                                dve.wait_ge(r.gathered[c], 16 * ct * (base + i + 1))
                                g = G[:, c, 0:ct * CELL_W].rearrange("p (a f) -> p a f", f=F)
                                w = COEF[:, bass.ds(at * 4, ct * 4)]
                                v.tensor_tensor(g, g, bc(w, [P, ct * 4, F]), ALU.mult).then_inc(r.prod_ready, 1)
                            if kind == "mlp" and not r.fast:
                                add_rows(i, c)
                            elif kind == "mlp" and c > 0:
                                add_rows(i, c - 1)
                            elif kind == "mlp" and not first:
                                add_rows(i - 1, r.chunks - 1)
                    if n == 0 and not r.fast:
                        with dve.Fori(0, z.tiles) as i:
                            link = Links(dve, sem("slots_dve"), i, 7)
                            col = DSTF[:, bass.ds(i, 1)]
                            hold(dve)
                            v.tensor_copy(ROWS[:, :], col.to_broadcast([P, P])).then_inc(sem("tile_staged"), 1)
                            dve.wait_ge(sem("tile_row"), i + 1)
                            link(v.tensor_tensor(OH[:, 0, 0, :], ROW, col.to_broadcast([P, P]), ALU.is_equal))
                            link(v.tensor_tensor(OH[:, 0, 0, :], OH[:, 0, 0, :], LOWER[:, :], ALU.mult))
                            link(v.tensor_reduce(SMALL[:, 0:1], OH[:, 0, 0, :], AX.X, ALU.add))
                            link(v.tensor_scalar(SMALL[:, 0:1], SMALL[:, 0:1], 0.0, None, ALU.is_gt))
                            link(v.tensor_tensor(SMALL[:, 1:2], TRASH[:, :], col, ALU.subtract))
                            link(v.scalar_tensor_tensor(out=SLOTF[:, bass.ds(i, 1)], in0=SMALL[:, 1:2],
                                                        scalar=SMALL[:, 0:1], in1=col, op0=ALU.mult, op1=ALU.add))
                            hold(dve)
                            link(v.tensor_copy(SLOTI[:, bass.ds(i, 1)], SLOTF[:, bass.ds(i, 1)]))
                            link.end()
                    over_groups(dve, r, body)
                    if kind == "mlp" and r.fast:
                        add_rows(r.groups - 1, r.chunks - 1)
                per_route(dve, flag, run)

            def norm_stage(k):
                link = Links(dve, sem("n0_link"), k, 8)
                norm("n0", k, link)
                stage("n0", k, 0, part(H, k))
                link.end()

            def n0(k, last):
                cells("n0", k, None if last else lambda: norm_stage(k + 1))
                finish("n0")
            norm_stage(0)
            n0(0, False)
            with dve.Fori(1, z.steps - 1) as k:
                n0(k, False)
            n0(z.steps - 1, True)
            dve.wait_ge(phase_done, 1)
            run_pass(0)
            dve.wait_ge(pass_done, 1)

            dve.wait_ge(sem("s17_in"), 16)
            count[0] = 0
            deg = sem("degree_dve")

            def dlink(instruction):
                count[0] += 1
                instruction.then_inc(deg, 1)
                dve.wait_ge(deg, count[0])
            dlink(v.tensor_scalar(INVD[:, :], S17[:, :, 16], 1.0, None, ALU.max))
            dlink(v.reciprocal(INVD[:, :], INVD[:, :]))
            v.tensor_copy(SMALL[:, 3:4], PIDX[:, :]).then_inc(sem("invdeg_ready"), 1)
            dve.wait_ge(sem("invroot_ready"), 1)
            dlink(v.scalar_tensor_tensor(out=DINV[:, :], in0=S17[:, :, 16], scalar=0.0, in1=DINV[:, :],
                                         op0=ALU.is_gt, op1=ALU.mult))

            def spline_out(ph, k, link):
                stage(ph, k, 0, part(H, k))
                dve.wait_ge(sem("sums_in"), since(ph, "sums_in") + 16 * (k + 1))
                parts = AG[:, :].rearrange("p (b s f) -> p b f s", s=4, f=F)
                link(v.tensor_reduce(XC[:, :, :], parts, AX.X, ALU.add))
                link(v.tensor_tensor(XC[:, :, :], XC[:, :, :], bc(part(INVD, k), NF), ALU.mult))
                dve.wait_ge(sem(f"{ph}_rf_ps"), k + 1)
                rf = PS[:, R0 * 512:R0 * 512 + NB_STEP * 2 * F].rearrange("p (b w) -> p b w", w=2 * F)
                link(v.tensor_tensor(XC[:, :, :], XC[:, :, :], rf[:, :, 0:F], ALU.add))
                link(v.tensor_scalar(part(H, k), XC[:, :, :], 0.0, None, ALU.max))
                link(v.tensor_tensor(part(X, k), part(X, k), rf[:, :, F:2 * F], ALU.add))

            def n1(k, first):
                link = Links(dve, sem("n1_link"), k, 5)
                spline_out("n1", k, link)
                v.tensor_copy(SMALL[:, 3:4], PIDX[:, :]).then_inc(sem("sums_used"), 1)
                stage("n1", k, 1, part(H, k))
                cells("n1", k)
                finish("n1")
                link.end()
            over_steps(n1)
            dve.wait_ge(phase_done, 2)
            run_pass(1)
            dve.wait_ge(pass_done, 2)

            def n2(k, first):
                link = Links(dve, sem("n2_link"), k, 14)
                spline_out("n2", k, link)
                v.tensor_copy(SMALL[:, 3:4], PIDX[:, :]).then_inc(sem("sums_used"), 1)
                stage("n2", k, 1, part(H, k))
                dve.wait_ge(sem("n2_f_ps"), k + 1)
                f = PS[:, 6 * 512:6 * 512 + NB_STEP * F].rearrange("p (b w) -> p b w", w=F)
                link(v.tensor_tensor(part(X, k), part(X, k), f, ALU.add))
                if not first:
                    dve.wait_ge(sem("n2_rows_stored"), 16 * k)
                norm("n2", k, link)
                v.tensor_tensor(SQ[:, :, :], part(H, k), bc(part(DINV, k), NF), ALU.mult).then_inc(sem("n2_rows_ready"), 1)
                finish("n2")
                link.end()
            over_steps(n2)
            dve.wait_ge(phase_done, 3)
            run_pass(2)
            dve.wait_ge(pass_done, 3)

            def n3(k, first):
                link = Links(dve, sem("n3_link"), k, 10)
                dve.wait_ge(sem("sums_in"), since("n3", "sums_in") + 16 * (k + 1))
                link(v.tensor_tensor(XC[:, :, :], sums(F), bc(part(DINV, k), NF), ALU.mult))
                link(v.tensor_tensor(part(X, k), part(X, k), XC[:, :, :], ALU.add))
                v.tensor_copy(SMALL[:, 3:4], PIDX[:, :]).then_inc(sem("sums_used"), 1)
                norm("n3", k, link)
                if not first:
                    dve.wait_ge(sem("turned"), since("n3", "turned") + k)
                stage("n3", k, 0, part(H, k))
                finish("n3")
                link.end()
            over_steps(n3)
            dve.wait_ge(phase_done, 4)
            run_pass(3)
            dve.wait_ge(pass_done, 4)

            def update_inputs(k, link):
                link(v.tensor_copy(ST[:, :, 0:F], part(H, k)))
                hold(dve)
                link(v.tensor_copy(TINY[:, 4, :], part(S17, k)[:, :, 16]))
                link(v.tensor_tensor(XC[:, :, :], MB2[:, :].unsqueeze(1).to_broadcast(NF), bc(TINY[:, 4, :], NF),
                                     ALU.mult))
                dve.wait_ge(sem("n4_agg_ps"), k + 1)
                v.tensor_copy(SMALL[:, 3:4], PIDX[:, :]).then_inc(sem("sums_used"), 1)
                agg = PS[:, R0 * 512:R0 * 512 + NB_STEP * F].rearrange("p (b w) -> p b w", w=F)
                link(v.tensor_tensor(ST[:, :, F:2 * F], agg, XC[:, :, :], ALU.add))
                v.tensor_copy(SMALL[:, 3:4], PIDX[:, :]).then_inc(sem("stage1"), 1)

            def n4(k, last):
                link = Links(dve, sem("n4_link"), k, 13)
                dve.wait_ge(sem("n4_y_ps"), k + 1)
                y = PS[:, 6 * 512:6 * 512 + NB_STEP * F].rearrange("p (b w) -> p b w", w=F)
                link(v.tensor_tensor(part(X, k), part(X, k), y, ALU.add))
                if last:
                    for _ in range(4):
                        link(v.tensor_copy(SMALL[:, 3:4], PIDX[:, :]))
                else:
                    update_inputs(k + 1, link)
                v.tensor_tensor(part(X, k), part(X, k), UB2[:, :].unsqueeze(1).to_broadcast(NF), ALU.add
                                ).then_inc(sem("n4_updated"), 1)
                dve.wait_ge(sem("n4_updated"), k + 1)
                norm("n4", k, link)
                finish("n4")
            flink = Links(dve, sem("n4_first"), 0, 4)
            update_inputs(0, flink)
            with dve.Fori(0, z.steps - 1) as k:
                n4(k, False)
            n4(z.steps - 1, True)

            for l in range(3):
                dve.wait_ge(phase_done, 5 + l)
                run_pass(4 + l)
                dve.wait_ge(pass_done, 5 + l)
                ph = f"n{5 + l}"

                def stage_inputs(k, first):
                    link = Links(dve, sem(f"{ph}_link"), k, 2)
                    link(v.tensor_scalar(TINY[:, 4, :], part(S17, k)[:, :, 16], 1.0, None, ALU.add))
                    if not first:
                        dve.wait_ge(sem("turned"), since(ph, "turned") + 2 * k)
                    link(v.tensor_tensor(ST[:, :, 0:F], part(H, k), bc(TINY[:, 4, :], NF), ALU.mult))
                    dve.wait_ge(sem("sums_in"), since(ph, "sums_in") + 16 * (k + 1))
                    v.tensor_tensor(ST[:, :, F:2 * F], part(H, k), sums(F), ALU.add).then_inc(sem("stage0"), 1)
                    v.tensor_copy(SMALL[:, 3:4], PIDX[:, :]).then_inc(sem("sums_used"), 1)
                    v.tensor_scalar(XC[:, :, 0:CAT_E], part(S17, k), 1.0, None, ALU.add).then_inc(sem("stage1"), 1)

                def outputs(k):
                    dve.wait_ge(sem(f"{ph}_m_ps"), k + 1)
                    m = PS[:, R0 * 512:R0 * 512 + NB_STEP * F].rearrange("p (b w) -> p b w", w=F)
                    v.tensor_scalar(SQ[:, :, :], m, 0.0, None, ALU.max).then_inc(sem(f"{ph}_relu"), 1)
                    dve.wait_ge(sem(f"{ph}_relu"), k + 1)
                    if l < 2:
                        v.tensor_tensor(part(H, k), SQ[:, :, :], bc(part(MASK, k), NF), ALU.mult
                                        ).then_inc(sem("dve"), 1)
                    else:
                        v.tensor_tensor(part(X, k), part(X, k), SQ[:, :, :], ALU.add).then_inc(sem("dve"), 1)

                stage_inputs(0, True)
                with dve.Fori(0, z.steps - 1) as k:
                    stage_inputs(k + 1, False)
                    outputs(k)
                outputs(z.steps - 1)
                if l == 2:
                    break
                dve.wait_ge(sem("dve"), since(ph, "dve") + z.steps)
                blink = Links(dve, sem(f"{ph}_bn"), 0, 13)
                all_nf = [P, z.blocks, F]
                by_f = "p b f -> p f b"
                v.tensor_reduce(STAT[:, 0, :], H[:, :, :].rearrange(by_f), AX.X, ALU.add
                                ).then_inc(sem(f"{ph}_colsum"), 1)
                dve.wait_ge(sem(f"{ph}_total"), 1)
                blink(v.tensor_scalar(STAT[:, 1, :], bank(7, F), 1.0 / z.nodes, None, ALU.mult))
                blink(v.tensor_tensor(H[:, :, :], H[:, :, :], STAT[:, 1, :].unsqueeze(1).to_broadcast(all_nf),
                                      ALU.subtract))
                blink(v.tensor_tensor(D, H[:, :, :], bc(MASK[:, :], all_nf), ALU.mult))
                blink(v.tensor_tensor(D, D, D, ALU.mult))
                v.tensor_reduce(STAT[:, 0, :], D.rearrange(by_f), AX.X, ALU.add).then_inc(sem(f"{ph}_colsum"), 1)
                dve.wait_ge(sem(f"{ph}_total"), 2)
                blink(v.tensor_scalar(STAT[:, 2, :], bank(7, F), 1.0 / z.nodes, EPS, ALU.mult, ALU.add))
                v.reciprocal(STAT[:, 2, :], STAT[:, 2, :]).then_inc(sem(f"bn{l}_var"), 1)
                dve.wait_ge(sem(f"bn{l}_rstd"), 1)
                blink(v.tensor_tensor(STAT[:, 3, :], STAT[:, 3, :], GAM[:, l, :], ALU.mult))
                blink(v.tensor_tensor(H[:, :, :], H[:, :, :], STAT[:, 3, :].unsqueeze(1).to_broadcast(all_nf),
                                      ALU.mult))
                blink(v.tensor_tensor(H[:, :, :], H[:, :, :], BET[:, l, :].unsqueeze(1).to_broadcast(all_nf),
                                      ALU.add))
                v.tensor_scalar(H[:, :, :], H[:, :, :], 0.0, None, ALU.max).then_inc(sem(f"{ph}_normed"), 1)



def kernel(**inputs):
    import numpy as np
    import concourse.bacc as bacc
    from concourse.bass_utils import run_bass_kernel_spmd

    a = {n: np.asarray(v) for n, v in inputs.items()}
    nodes, edges = a["x"].shape[0], a["src"].shape[0]
    z = Sizes(nodes, edges)
    padded = z.tiles * P

    def by_tile(v, fill):
        v = v.reshape(edges, -1)
        full = np.full((padded, v.shape[1]), fill, v.dtype)
        full[:edges] = v
        return np.ascontiguousarray(full.reshape(z.groups, P, TILES, -1).transpose(1, 0, 2, 3)
                                    .reshape(P, z.tiles, -1))

    x = np.zeros((z.rows, F), np.float32)
    x[:nodes] = a["x"]
    ea17 = np.ones((P, z.tiles, CAT_E), np.float32)
    ea17[:, :, :16] = by_tile(a["edge_attr_16"], 0)
    w = {
        "x": x, "dst": by_tile(a["dst"], nodes)[:, :, 0], "src": by_tile(a["src"], 0)[:, :, 0],
        "ea2": by_tile(a["edge_attr_2"], 0).reshape(P, -1), "ea17": ea17,
        "ef": by_tile(a["edge_attr_32"], 0).transpose(2, 1, 0).reshape(FEAT_E, -1),
        "roots": a["L0_gnn_roots"], "biases": a["L0_gnn_biases"], "fw": a["L0_gnn_final_w"].T,
        "fb": a["L0_gnn_final_b"][None], "mw1": a["L2_gnn_mW1"], "mb1": a["L2_gnn_mb1"][None],
        "mw2": a["L2_gnn_mW2"], "mb2": a["L2_gnn_mb2"][None], "uw1": a["L2_gnn_uW1"],
        "ub1": a["L2_gnn_ub1"][:, None], "uw2": a["L2_gnn_uW2"], "ub2": a["L2_gnn_ub2"][None],
    }
    for l in range(2):
        w[f"wk{l}"] = a["L0_gnn_weights"][l].transpose(1, 0, 2).reshape(F, 25 * F)
        w[f"g{l}"], w[f"be{l}"] = a[f"L3_gnn_g{l}"][None], a[f"L3_gnn_be{l}"][None]
    for l in range(3):
        w[f"w{l}"], w[f"b{l}"] = a[f"L3_gnn_W{l}"].T, a[f"L3_gnn_b{l}"][None]

    nc = bacc.Bacc("TRN2", target_bir_lowering=False, num_devices=1)
    arrays = {f"in_{n}": np.ascontiguousarray(v) for n, v in w.items()}
    t = {n: nc.dram_tensor(f"in_{n}", arrays[f"in_{n}"].shape, mybir.dt.from_np(arrays[f"in_{n}"].dtype),
                           kind="ExternalInput").ap() for n in w}
    t["out"] = nc.dram_tensor("out", (z.rows, F), F32, kind="ExternalOutput").ap()
    gnn_program(nc, z, t)
    r = run_bass_kernel_spmd(nc, [arrays], core_ids=[0])
    return r.results[0]["out"][:nodes]
```
